# Optimizing a Trainium2 kernel written in Bass

```python
import numpy as np
import jax
import jax.numpy as jnp

def _softmax(x, axis=-1):
    return jax.nn.softmax(x, axis=axis)

def _gelu(x):
    return jax.nn.gelu(x, approximate=True)

def _silu(x):
    return jax.nn.silu(x)

def _sigmoid(x):
    return jax.nn.sigmoid(x)

def _layernorm(x, axis=-1, eps=1e-05):
    m = jnp.mean(x, axis=axis, keepdims=True)
    v = jnp.var(x, axis=axis, keepdims=True)
    return (x - m) / jnp.sqrt(v + eps)

def _scatter_add(tgt, idx, src, axis=0):
    return tgt.at[idx].add(src)

def _segment_sum(src, seg, n):
    return jax.ops.segment_sum(src, seg, n)
kernel_name = 'mk_conv_preact_d1_conv_nchw256_r2_e9e849'

def setup_inputs(seed: int=0):
    np.random.seed(seed)
    _w = jnp.asarray

    def _rec_inputs():
        import jax
        import jax.numpy as jnp
        _gk = jax.random.key(seed)
        x = -8.268e-05 + 0.9999 * jax.random.normal(jax.random.fold_in(_gk, 1), (4, 128, 112, 112), jnp.float32)
        return x
    x = _rec_inputs()

    def _L0_conv_setup():
        import jax, jax.numpy as jnp
        import numpy as np
        WS = 7
        HEADS = 8
        SHIFT = WS // 2
        key = jax.random.key(seed)
        k1, k2, k3 = jax.random.split(key, 3)
        B, C, H, W = (4, 128, 112, 112)
        x = jax.random.normal(k1, (B, C, H, W), dtype=jnp.float32)
        w_qkv = jax.random.normal(k2, (3 * C, C), dtype=jnp.float32) * (1.0 / np.sqrt(C))
        b_qkv = jax.random.normal(k3, (3 * C,), dtype=jnp.float32) * 0.02
        return {'x': x, 'w_qkv': w_qkv, 'b_qkv': b_qkv}
    _L0_conv_all = _L0_conv_setup()
    _L0_conv_in = {k: v for k, v in _L0_conv_all.items() if k in ('w_qkv', 'b_qkv')}
    del _L0_conv_all
    return {'x': x, 'L0_conv_w_qkv': _L0_conv_in['w_qkv'], 'L0_conv_b_qkv': _L0_conv_in['b_qkv']}

def reference(x, L0_conv_w_qkv, L0_conv_b_qkv):
    import jax
    import jax.numpy as jnp

    def _L0_conv_ref(x, w_qkv, b_qkv):
        import jax, jax.numpy as jnp
        import numpy as np
        WS = 7
        HEADS = 8
        SHIFT = WS // 2
        B, C, H, W = x.shape
        hd = C // HEADS
        Hn, Wn = (H // WS, W // WS)
        xs = jnp.roll(x, (-SHIFT, -SHIFT), axis=(-2, -1))
        qkv = jnp.einsum('bchw,oc->bohw', xs, w_qkv) + b_qkv[None, :, None, None]
        w = qkv.reshape(B, 3, HEADS, hd, Hn, WS, Wn, WS)
        w = jnp.transpose(w, (1, 0, 4, 6, 2, 5, 7, 3))
        w = w.reshape(3, B, Hn, Wn, HEADS, WS * WS, hd)
        q, k, v = (w[0], w[1], w[2])
        scale = 1.0 / np.sqrt(hd)
        scores = jnp.einsum('bxyhqd,bxyhkd->bxyhqk', q, k) * scale
        attn = jax.nn.softmax(scores, axis=-1)
        out = jnp.einsum('bxyhqk,bxyhkd->bxyhqd', attn, v)
        out = out.reshape(B, Hn, Wn, HEADS, WS, WS, hd)
        out = jnp.transpose(out, (0, 3, 6, 1, 4, 2, 5))
        out = out.reshape(B, C, H, W)
        out = jnp.roll(out, (SHIFT, SHIFT), axis=(-2, -1))
        return out

    def _gn(v, G=32, eps=1e-05):
        B_, C_, H_, W_ = v.shape
        g = v.reshape(B_, G, C_ // G, H_, W_)
        m = jnp.mean(g, axis=(2, 3, 4), keepdims=True)
        s = jnp.var(g, axis=(2, 3, 4), keepdims=True)
        return ((g - m) / jnp.sqrt(s + eps)).reshape(v.shape)

    def _ln_c(v, eps=1e-06):
        m = jnp.mean(v, axis=1, keepdims=True)
        s = jnp.var(v, axis=1, keepdims=True)
        return (v - m) / jnp.sqrt(s + eps)

    def _ln_t(v, eps=1e-05):
        m = jnp.mean(v, axis=-1, keepdims=True)
        s = jnp.var(v, axis=-1, keepdims=True)
        return (v - m) / jnp.sqrt(s + eps)

    def _to_tokens(v):
        B_, C_, H_, W_ = v.shape
        return v.reshape(B_, C_, H_ * W_).transpose(0, 2, 1)

    def _from_tokens(t, like):
        B_, C_, H_, W_ = like.shape
        return t.transpose(0, 2, 1).reshape(B_, C_, H_, W_)
    x = x + _L0_conv_ref(_gn(x), L0_conv_w_qkv, L0_conv_b_qkv)
    return x

_drawn_inputs = setup_inputs


def setup_inputs(seed=0):
    import zlib

    import numpy as np

    out = dict(_drawn_inputs(seed))
    spreads = {}
    factors = {}
    for name, (base, spread) in spreads.items():
        noise = np.random.default_rng([zlib.crc32(name.encode()), seed]).standard_normal(out[name].shape)
        drawn = base * np.exp(spread * noise) if base else spread * noise
        out[name] = jnp.asarray(drawn.astype(out[name].dtype))
    for name, factor in factors.items():
        out[name] = (out[name] * factor).astype(out[name].dtype)
    return out
```

```python
import numpy as np

import concourse.bass as bass
from concourse import mybir
from contextlib import ExitStack

B, C, H, W = 4, 128, 112, 112
WS, SHIFT, HEADS, GN_GROUPS = 7, 3, 8, 32
HD = C // HEADS
PER = C // GN_GROUPS
EPS = 1e-5
TOK = WS * WS
BANDS = H // WS
NW = W // WS
GW = NW // 2
GT = GW * TOK
PAIRS = GW // 2
HP = HEADS // 2
PC = 2 * HD
ROWS2 = 2 * TOK
PITCH = 64
KROWS = PITCH + TOK
BAND = WS * W
SLOTS = 2 * BANDS
GROUPS = B * BANDS * 2
STAT = 448
CHUNKS = H * W // STAT
Q_LEN = GW * ROWS2
Q_PAD = 128 - ROWS2
NEWTON = 4
AGG = 14 + 4 * NEWTON
HEADROOM = 128.0


def window_attention(nc, x, w_qkv, b_qkv, out):
    f32, f16, i32 = mybir.dt.float32, mybir.dt.float16, mybir.dt.int32
    ALU, ACT, AX = mybir.AluOpType, mybir.ActivationFunctionType, mybir.AxisListType

    x_v = x.rearrange("b c h w -> b c (h w)")
    out_v = out.rearrange("b c h w -> b c (h w)")

    ctx = ExitStack()
    with ctx:
        def sb(name, shape, dt=f32):
            return ctx.enter_context(nc.sbuf_tensor(name, shape, dt))

        def sem(name):
            return ctx.enter_context(nc.semaphore(name))

        image = sb("image", [C, SLOTS * BAND])
        xn = sb("xn", [C, 2, GW, PITCH])
        k32 = sb("k32", [C, GT])
        q32 = sb("q32", [C, GW, 2, TOK])
        k_hi, k_lo = sb("k_hi", [C, 2, GT], f16), sb("k_lo", [C, 2, GT], f16)
        q_hi, q_lo = sb("q_hi", [C, 2, Q_LEN + Q_PAD], f16), sb("q_lo", [C, 2, Q_LEN + Q_PAD], f16)
        row_max = sb("row_max", [ROWS2, 2, 2, GW])
        shifted = sb("shifted", [ROWS2, 2, 2, GW, TOK])
        probs = sb("probs", [ROWS2, 2, HP, GW, PITCH])
        probs_t = sb("probs_t", [KROWS, 2, HP, ROWS2])
        v_rows = sb("v_rows", [KROWS, 2, PAIRS, HP, 2, PC + 1])
        inv_sum = sb("inv_sum", [ROWS2, 2, HP * 2])
        mixed = sb("mixed", [ROWS2, PAIRS, 2, HP, PC])
        even_out = sb("even_out", [C, GW // 2, TOK])
        both_out = sb("both_out", [C, 2, GW, TOK])
        stage = sb("stage", [C, 2 * BAND])
        w_nat = sb("w_nat", [C, 3, C])
        w_t = sb("w_t", [C, 3, C])
        bias = sb("bias", [C, 3])
        ident = sb("ident", [C, C])
        head_of = sb("head_of", [C, HEADS])
        even_odd = sb("even_odd", [C, 2])
        size = sb("size", [C, 2])
        size_b = sb("size_b", [C, 2])
        size_all = sb("size_all", [C, 2])
        fit = sb("fit", [C, 2])
        q_scale, q_bias = sb("q_scale", [C, 2]), sb("q_bias", [C, 2])
        k_bias = sb("k_bias", [C, 1])
        exp_scale = sb("exp_scale", [C, 1])
        stats = sb("stats", [C, CHUNKS, 6])
        mean_blk, var_blk = sb("mean_blk", [C, 32]), sb("var_blk", [C, 32])
        mean_row, var_row = sb("mean_row", [C, 32]), sb("var_row", [C, 32])
        work_a, work_b = sb("work_a", [C, 32]), sb("work_b", [C, 32])
        g_mean, g_var, rs, rs_t = (sb(n, [C, 8]) for n in ("g_mean", "g_var", "rs", "rs_t"))
        half_bits = sb("half_bits", [C, 8], i32)
        agg = sb("agg", [C, 2])
        mean_c, rstd_c = sb("mean_c", [C, 32]), sb("rstd_c", [C, 32])

        psum = ctx.enter_context(nc.psum_tensor("psum", [128, 8, 512], f32))
        S_BANKS, T_BANKS, PV_BANKS = slice(0, 2), (3, 2), (4, 5)
        K_BANK, Q_BANK, V_BANK, BACK_BANKS = 2, 6, 7, (6, 7)

        loaded0 = [sem(f"loaded_first_{n}") for n in range(4)]
        loaded = [None] + [sem(f"loaded_image_{b}") for b in range(1, B)]
        w_loaded, stored = sem("w_loaded"), sem("stored")
        consts, sized, w_transposed, w_ready, ready = (sem(n) for n in ("consts", "sized", "w_transposed", "w_ready", "ready"))
        pool_chain, dve_chain, agg_chain = sem("pool_chain"), sem("dve_chain"), sem("agg_chain")
        stats_done, waited, waited_sp = sem("stats_done"), sem("waited"), sem("waited_sp")
        xn_ready, q_mm, k_mm, v_mm = sem("xn_ready"), sem("q_mm"), sem("k_mm"), sem("v_mm")
        q_evac, k_evac, v_evac = sem("q_evac"), sem("k_evac"), sem("v_evac")
        k_high, q_high, k_split, q_split = sem("k_high"), sem("q_high"), sem("k_split"), sem("q_split")
        s_mm = [sem("s_mm_0"), sem("s_mm_1")]
        max_done = [sem("max_done_0"), sem("max_done_1")]
        sub_done = [sem("sub_done_0"), sem("sub_done_1")]
        exp_done = [sem("exp_done_0"), sem("exp_done_1")]
        pt_mm, pt_evac, pv_mm = sem("pt_mm"), sem("pt_evac"), sem("pv_mm")
        inv_done, norm_done = sem("inv_done"), sem("norm_done")
        back_mm, even_done, both_done, add_done = sem("back_mm"), sem("even_done"), sem("both_done"), sem("add_done")

        def wait(engine, semaphore, count):
            if not isinstance(count, int) or count > 0:
                engine.wait_ge(semaphore, count)

        def in_windows(flat, first, n):
            rows = flat.rearrange("p (r c) -> p r c", c=W)[:, :, first:first + n * WS]
            return rows.rearrange("p r (w c) -> p w r c", c=WS)

        def pieces(half):
            if half == 0:
                return [(0, GW, 0, WS, SHIFT)]
            first = SHIFT + GW * WS
            return [(0, GW - 1, 0, WS, first), (GW - 1, 1, 0, WS - SHIFT, W - (WS - SHIFT)), (GW - 1, 1, WS - SHIFT, SHIFT, 0)]

        def token_view(tokens, piece):
            w0, n, c0, nc_, _ = piece
            return tokens[:, w0:w0 + n, :].rearrange("p w (r c) -> p w r c", c=WS)[:, :, :, c0:c0 + nc_]

        def pixel_view(flat, piece):
            w0, n, c0, nc_, first = piece
            if n > 1:
                return in_windows(flat, first, n)
            rows = flat.rearrange("p (r c) -> p r c", c=W)[:, :, first:first + nc_]
            return rows.rearrange("p r (w c) -> p w r c", c=nc_)

        block = ctx.enter_context(nc.Block())

        @block.sync
        def _(sp):
            sp.dma_start(w_nat[:, :, :], w_qkv.rearrange("(j o) c -> o j c", j=3)).then_inc(w_loaded, 16)
            sp.dma_start(bias[:, :], b_qkv.rearrange("(j o) -> o j", j=3), allow_slow_non_contiguous=True).then_inc(w_loaded, 16)

            def load_rows(b, row, n, semaphore, slot_row):
                sp.dma_start(image[:, slot_row * W:(slot_row + n) * W],
                             x_v[b, :, row * W:(row + n) * W]).then_inc(semaphore, 16)

            quarter = H // 4
            for n in range(3):
                load_rows(0, n * quarter + SHIFT, quarter, loaded0[n], n * quarter)
            load_rows(0, 3 * quarter + SHIFT, quarter - SHIFT, loaded0[3], 3 * quarter)
            load_rows(0, 0, SHIFT, loaded0[3], H - SHIFT)
            load_rows(1, SHIFT, H - SHIFT, loaded[1], H)
            load_rows(1, 0, SHIFT, loaded[1], 2 * H - SHIFT)

            def store_band(b, y):
                t = b * BANDS + y
                sp.wait_ge(add_done, 2 * t + 2)
                sp.sem_inc(waited_sp, 1)
                at = (y & 1) * BAND
                top = (WS - SHIFT) * W
                src = stage[:, bass.ds(at, BAND)]
                sp.dma_start(out_v[bass.ds(b, 1), :, bass.ds((y * WS + SHIFT) * W, top)].rearrange("b c n -> c (b n)"),
                             src[:, 0:top]).then_inc(stored, 16)
                sp.dma_start(out_v[bass.ds(b, 1), :, bass.ds(((y + 1) & (BANDS - 1)) * BAND, BAND - top)]
                             .rearrange("b c n -> c (b n)"), src[:, top:BAND]).then_inc(stored, 16)

            def load_band(b_static, y):
                at = (b_static % 2) * BANDS * BAND + y * BAND
                top = (WS - SHIFT) * W
                slot = image[:, bass.ds(at, BAND)]
                sp.dma_start(slot[:, 0:top], x_v[b_static, :, bass.ds((y * WS + SHIFT) * W, top)]).then_inc(loaded[b_static], 16)
                sp.dma_start(slot[:, top:BAND], x_v[b_static, :, bass.ds(((y + 1) & (BANDS - 1)) * BAND, BAND - top)]
                             ).then_inc(loaded[b_static], 16)

            def wait_stored(b, y):
                sp.wait_ge(stored, 32 * (b * BANDS + y) + 32)
                sp.sem_inc(waited_sp, 1)

            for b in range(2):
                with sp.Fori(0, BANDS) as y:
                    store_band(b, y)
                    load_band(b + 2, y)
                    sp.wait_ge(loaded[b + 2], 32 * y + 32)
                    wait_stored(b, y)
            with sp.Fori(2, B) as b:
                with sp.Fori(0, BANDS) as y:
                    store_band(b, y)
                    wait_stored(b, y)

        @block.gpsimd
        def _(pool):
            nc.gpsimd.memset(ident[:, :], 0.0).then_inc(pool_chain, 1)
            nc.gpsimd.memset(head_of[:, :], 1.0).then_inc(pool_chain, 1)
            pool.wait_ge(pool_chain, 2)
            nc.gpsimd.affine_select(out=ident[:, :], in_=ident[:, :], compare_op=ALU.not_equal, fill=1.0, base=0,
                                    pattern=[[-1, C]], channel_multiplier=1).then_inc(consts, 1)
            nc.gpsimd.affine_select(out=head_of[:, :], in_=head_of[:, :], compare_op=ALU.is_ge, fill=0.0, base=0,
                                    pattern=[[-HD, HEADS]], channel_multiplier=1).then_inc(pool_chain, 1)
            pool.wait_ge(pool_chain, 3)
            nc.gpsimd.affine_select(out=head_of[:, :], in_=head_of[:, :], compare_op=ALU.is_ge, fill=0.0, base=HD - 1,
                                    pattern=[[HD, HEADS]], channel_multiplier=-1).then_inc(consts, 1)
            nc.gpsimd.memset(probs[:, :, :, :, TOK:PITCH], 0.0).then_inc(consts, 1)
            nc.gpsimd.memset(q_hi[:, :, Q_LEN:], 0.0).then_inc(consts, 1)
            nc.gpsimd.memset(q_lo[:, :, Q_LEN:], 0.0).then_inc(consts, 1)
            nc.gpsimd.memset(v_rows[:, :, :, :, :, :], 0.0).then_inc(pool_chain, 1)
            pool.wait_ge(pool_chain, 4)
            nc.gpsimd.memset(v_rows[0:TOK, :, :, :, 0, PC:PC + 1], 1.0).then_inc(consts, 1)
            nc.gpsimd.memset(v_rows[PITCH:KROWS, :, :, :, 1, PC:PC + 1], 1.0).then_inc(consts, 1)
            pool.wait_ge(sized, 1)
            pool.wait_ge(consts, 7)
            nc.gpsimd.partition_all_reduce(size_all[:, :], size[:, :], C, bass.bass_isa.ReduceOp.max).then_inc(consts, 1)

            def split(g, par):
                pool.wait_ge(k_evac, g + 1)
                wait(pool, s_mm[1], g - 1)
                pool.sem_inc(waited, 1)
                nc.gpsimd.tensor_scalar(k_hi[:, par, :], k32[:, :], 1.0, 0.0, ALU.mult, ALU.add).then_inc(k_high, 1)
                pool.wait_ge(k_high, g + 1)
                nc.gpsimd.tensor_tensor(k_lo[:, par, :], k32[:, :], k_hi[:, par, :], ALU.subtract).then_inc(k_split, 1)
                pool.wait_ge(q_evac, g + 1)
                q_flat = q32[:, :, :, :].rearrange("p w e q -> p (w e q)")
                pool.sem_inc(waited, 1)
                nc.gpsimd.tensor_scalar(q_hi[:, par, 0:Q_LEN], q_flat, 1.0, 0.0, ALU.mult, ALU.add).then_inc(q_high, 1)
                pool.wait_ge(q_high, g + 1)
                nc.gpsimd.tensor_tensor(q_lo[:, par, 0:Q_LEN], q_flat, q_hi[:, par, 0:Q_LEN], ALU.subtract).then_inc(q_split, 1)

            def add_image(g, t, half):
                pool.wait_ge(both_done, 2 * g + 2)
                if half == 0:
                    wait(pool, stored, 32 * (t - 1))
                at, st = (t & (SLOTS - 1)) * BAND, (t & 1) * BAND
                for piece in pieces(half):
                    last = nc.gpsimd.tensor_tensor(pixel_view(stage[:, bass.ds(st, BAND)], piece), token_view(both_out[:, half], piece),
                                                   pixel_view(image[:, bass.ds(at, BAND)], piece), ALU.add)
                last.then_inc(add_done, 1)

            split(0, 0)
            split(1, 1)
            split(2, 0)

            def two_steps(i):
                split(2 * i + 3, 1)
                add_image(2 * i, i, 0)
                split(2 * i + 4, 0)
                add_image(2 * i + 1, i, 1)

            two_steps(0)
            with pool.Fori(1, GROUPS // 2 - 2) as i:
                two_steps(i)
            split(GROUPS - 1, 1)
            for g in range(GROUPS - 4, GROUPS):
                add_image(g, g // 2, g % 2)

        @block.scalar
        def _(act):
            act.wait_ge(w_transposed, 1)
            nc.scalar.copy(w_t[:, :, :], psum[:, Q_BANK, 0:3 * C].rearrange("p (j o) -> p j o", j=3)).then_inc(w_ready, 1)
            act.wait_ge(ready, 1)

            def evac_qk(g):
                act.wait_ge(k_mm, g + 1)
                wait(act, k_split, g)
                nc.scalar.activation(k32[:, :], psum[:, K_BANK, 0:GT], ACT.Identity, bias=k_bias[:, 0:1],
                                     scale=fit[:, 1:2]).then_inc(k_evac, 1)
                act.wait_ge(q_mm, g + 1)
                wait(act, q_split, g)
                q = psum[:, Q_BANK, 0:GT].rearrange("p (w q) -> p w q", q=TOK)
                for e in range(2):
                    last = nc.scalar.activation(q32[:, :, e, :], q, ACT.Identity, bias=q_bias[:, e:e + 1],
                                                scale=q_scale[:, e:e + 1])
                last.then_inc(q_evac, 1)

            def evac_probs_t(c, p):
                act.wait_ge(pt_mm, 4 * c + p + 1)
                wait(act, pv_mm, 4 * c + p - 1)
                nc.scalar.copy(probs_t[:, p % 2, :, :], psum[0:KROWS, T_BANKS[p % 2], 0:HP * ROWS2]
                               .rearrange("p (h q) -> p h q", h=HP)).then_inc(pt_evac, 1)

            def evac_v(g, par):
                act.wait_ge(v_mm, g + 1)
                wait(act, pv_mm, 4 * (g - 1))
                v = psum[:, V_BANK, :].rearrange("p (a h d) -> p a h d", a=PAIRS, h=HP)
                nc.scalar.copy(v_rows[0:TOK, par, :, :, 0, 0:PC], v[0:TOK])
                nc.scalar.copy(v_rows[PITCH:KROWS, par, :, :, 1, 0:PC], v[PITCH:KROWS]).then_inc(v_evac, 1)

            def exp(g, par, j):
                act.wait_ge(sub_done[j], g + 1)
                wait(act, pt_mm, 4 * (g - 1))
                nc.scalar.activation(probs[:, par, 2 * j:2 * j + 2, :, 0:TOK], shifted[:, j, :, :, :], ACT.Exp,
                                     scale=exp_scale[0:ROWS2, 0:1]).then_inc(exp_done[j], 1)

            def evac_back(c, n):
                act.wait_ge(back_mm, 2 * c + n + 1)
                wait(act, both_done, 2 * c + n)
                back = psum[:, BACK_BANKS[n], 0:GW // 2 * ROWS2].rearrange("p (w e q) -> p w e q", e=2, q=TOK)
                nc.scalar.activation(even_out[:, :, :], back[:, :, 0, :], ACT.Identity, bias=bias[:, 2:3],
                                     scale=even_odd[:, 0:1]).then_inc(even_done, 1)

            def step(g, par, ahead=True, behind=2):
                if behind >= 2:
                    evac_back(g - 2, 1)
                if ahead:
                    evac_qk(g + 1)
                if behind:
                    evac_probs_t(g - 1, 0)
                    evac_probs_t(g - 1, 1)
                evac_v(g, par)
                exp(g, par, 0)
                if behind:
                    evac_probs_t(g - 1, 2)
                    evac_probs_t(g - 1, 3)
                exp(g, par, 1)
                if behind:
                    evac_back(g - 1, 0)

            evac_qk(0)
            step(0, 0, behind=0)
            step(1, 1, behind=1)
            step(2, 0)
            with act.Fori(1, GROUPS // 2 - 1) as i:
                step(2 * i + 1, 1)
                step(2 * i + 2, 0)
            step(GROUPS - 1, 1, ahead=False)
            evac_back(GROUPS - 2, 1)
            for p in range(PAIRS):
                evac_probs_t(GROUPS - 1, p)
            evac_back(GROUPS - 1, 0)
            evac_back(GROUPS - 1, 1)

        @block.vector
        def _(dve):
            chained = [0]

            def chain(instruction):
                chained[0] += 1
                instruction.then_inc(dve_chain, 1)
                dve.wait_ge(dve_chain, chained[0])

            chain(nc.vector.memset(mean_blk[:, :], 0.0))
            chain(nc.vector.memset(var_blk[:, :], 0.0))
            chain(nc.vector.memset(xn[:, :, :, TOK:PITCH], 0.0))
            dve.wait_ge(w_loaded, 32)
            chain(nc.vector.tensor_reduce(size[:, :], w_nat[:, 0:2, :], AX.X, ALU.add, apply_absolute_value=True))
            chain(nc.vector.tensor_reduce(size_b[:, :], bias[:, 0:2].rearrange("p (j o) -> p j o", o=1), AX.X, ALU.add,
                                          apply_absolute_value=True))
            nc.vector.tensor_tensor(size[:, :], size[:, :], size_b[:, :], ALU.add).then_inc(sized, 1)
            dve.wait_ge(consts, 8)
            chain(nc.vector.tensor_reduce(even_odd[:, :], head_of[:, :].rearrange("p (h e) -> p e h", e=2), AX.X, ALU.add))
            chain(nc.vector.tensor_scalar(size_all[:, :], size_all[:, :], 1e-18, 1.0 / HEADROOM, ALU.max, ALU.mult))
            chain(nc.vector.reciprocal(fit[:, :], size_all[:, :]))
            chain(nc.vector.tensor_scalar(q_scale[:, :], even_odd[:, :], fit[:, 0:1], None, ALU.mult))
            chain(nc.vector.tensor_scalar(q_bias[:, :], q_scale[:, :], bias[:, 0:1], None, ALU.mult))
            chain(nc.vector.tensor_scalar(k_bias[:, :], fit[:, 1:2], bias[:, 1:2], None, ALU.mult))
            nc.vector.tensor_scalar(exp_scale[:, :], size_all[:, 0:1], size_all[:, 1:2], float(HD) ** -0.5, ALU.mult,
                                    ALU.mult).then_inc(ready, 1)

            def take_stats(at, chunk):
                nc.vector.bn_stats(stats[:, bass.ds(chunk, 1), :].rearrange("p o s -> p (o s)"),
                                   image[:, bass.ds(at, STAT)]).then_inc(stats_done, 1)

            def aggregate(b):
                links = [0]

                def link(instruction):
                    links[0] += 1
                    instruction.then_inc(agg_chain, 1)
                    dve.wait_ge(agg_chain, b * AGG + links[0])

                def grouped(rows):
                    return rows[:, :].rearrange("p (g c) -> p g c", c=PER)

                dve.wait_ge(stats_done, CHUNKS * (b + 1))
                link(nc.vector.bn_aggr(agg[:, :], stats[:, :, :].rearrange("p n s -> p (n s)")))
                nc.vector.tensor_copy(mean_blk[:, 0:1], agg[:, 0:1])
                link(nc.vector.tensor_copy(var_blk[:, 0:1], agg[:, 1:2]))
                nc.vector.transpose(mean_row[:, :], mean_blk[:, :])
                link(nc.vector.transpose(var_row[:, :], var_blk[:, :]))
                link(nc.vector.tensor_reduce(g_mean[:, :], grouped(mean_row), AX.X, ALU.add))
                link(nc.vector.tensor_scalar(g_mean[:, :], g_mean[:, :], 1.0 / PER, None, ALU.mult))
                link(nc.vector.tensor_tensor(grouped(work_a), grouped(mean_row),
                                             g_mean[:, :, None].broadcast_to([C, 8, PER]), ALU.subtract))
                link(nc.vector.tensor_tensor(work_b[:, :], work_a[:, :], work_a[:, :], ALU.mult))
                link(nc.vector.tensor_tensor(work_a[:, :], work_b[:, :], var_row[:, :], ALU.add))
                link(nc.vector.tensor_reduce(g_var[:, :], grouped(work_a), AX.X, ALU.add))
                link(nc.vector.tensor_scalar(g_var[:, :], g_var[:, :], 1.0 / PER, EPS, ALU.mult, ALU.add))
                link(nc.vector.tensor_scalar(half_bits[:, :], g_var[:, :].bitcast(i32), 1, None, ALU.logical_shift_right))
                link(nc.vector.tensor_scalar(rs[:, :].bitcast(i32), half_bits[:, :], -1.0, float(0x5F3759DF), ALU.mult, ALU.add))
                for _ in range(NEWTON):
                    link(nc.vector.tensor_tensor(rs_t[:, :], rs[:, :], rs[:, :], ALU.mult))
                    link(nc.vector.tensor_tensor(rs_t[:, :], rs_t[:, :], g_var[:, :], ALU.mult))
                    link(nc.vector.tensor_scalar(rs_t[:, :], rs_t[:, :], -0.5, 1.5, ALU.mult, ALU.add))
                    link(nc.vector.tensor_tensor(rs[:, :], rs[:, :], rs_t[:, :], ALU.mult))
                nc.vector.tensor_copy(grouped(mean_row), g_mean[:, :, None].broadcast_to([C, 8, PER]))
                link(nc.vector.tensor_copy(grouped(var_row), rs[:, :, None].broadcast_to([C, 8, PER])))
                nc.vector.transpose(mean_c[:, :], mean_row[:, :])
                link(nc.vector.transpose(rstd_c[:, :], var_row[:, :]))
                assert links[0] == AGG

            def normalise(g, t, half):
                wait(dve, v_mm, g - 1)
                at = (t & (SLOTS - 1)) * BAND
                for piece in pieces(half):
                    last = nc.vector.tensor_scalar(token_view(xn[:, half, :, 0:TOK], piece),
                                                   pixel_view(image[:, bass.ds(at, BAND)], piece),
                                                   mean_c[:, 0:1], rstd_c[:, 0:1], ALU.subtract, ALU.mult)
                last.then_inc(xn_ready, 1)

            def maximum(g, j):
                dve.wait_ge(s_mm[j], g + 1)
                nc.vector.tensor_reduce(row_max[:, j, :, :], psum[0:ROWS2, S_BANKS, 0:GT]
                                        .rearrange("p h (w k) -> p h w k", k=TOK), AX.X, ALU.max).then_inc(max_done[j], 1)

            def subtract(g, j):
                dve.wait_ge(max_done[j], g + 1)
                wait(dve, exp_done[j], g)
                nc.vector.tensor_tensor(shifted[:, j, :, :, :], psum[0:ROWS2, S_BANKS, 0:GT]
                                        .rearrange("p h (w k) -> p h w k", k=TOK),
                                        row_max[:, j, :, :, None].broadcast_to([ROWS2, 2, GW, TOK]),
                                        ALU.subtract).then_inc(sub_done[j], 1)

            def divide(c, p):
                rows = psum[0:ROWS2, PV_BANKS[p % 2], 0:HP * 2 * (PC + 1)].rearrange("p (n d) -> p n d", d=PC + 1)
                dve.wait_ge(pv_mm, 4 * c + p + 1)
                nc.vector.reciprocal(inv_sum[:, p % 2, :], rows[:, :, PC]).then_inc(inv_done, 1)
                dve.wait_ge(inv_done, 4 * c + p + 1)
                wait(dve, back_mm, 2 * (c - 1) + p // 2 + 1)
                nc.vector.tensor_tensor(mixed[:, p, :, :, :].rearrange("p w h d -> p (w h) d"), rows[:, :, 0:PC],
                                        inv_sum[:, p % 2, :, None].broadcast_to([ROWS2, HP * 2, PC]), ALU.mult).then_inc(norm_done, 1)

            def join(c, par, n):
                dve.wait_ge(even_done, 2 * c + n + 1)
                wait(dve, add_done, c - 1)
                back = psum[:, BACK_BANKS[n], 0:GW // 2 * ROWS2].rearrange("p (w e q) -> p w e q", e=2, q=TOK)
                nc.vector.scalar_tensor_tensor(both_out[:, par, GW // 2 * n:GW // 2 * (n + 1), :], back[:, :, 1, :],
                                               even_odd[:, 1:2], even_out[:, :, :], ALU.mult, ALU.add).then_inc(both_done, 1)

            def step(g, t2, par, chunk=None, image_at=None, ahead=True, behind=2):
                maximum(g, 0)
                if behind >= 2:
                    join(g - 2, par, 1)
                subtract(g, 0)
                if chunk is not None:
                    take_stats(image_at + chunk * STAT, chunk)
                if ahead:
                    normalise(g + 2, t2, par)
                maximum(g, 1)
                if behind:
                    divide(g - 1, 0)
                subtract(g, 1)
                if behind:
                    for p in range(1, PAIRS):
                        divide(g - 1, p)
                    join(g - 1, 1 - par, 0)

            def two_steps(i, chunk=None, image_at=None, new_image=None):
                step(2 * i + 1, i + 1, 1, chunk, image_at)
                if new_image is not None:
                    aggregate(new_image)
                step(2 * i + 2, i + 2, 0, None if chunk is None else chunk + 1, image_at)

            for n in range(4):
                dve.wait_ge(loaded0[n], 16 if n < 3 else 32)
                with dve.Fori(n * CHUNKS // 4, (n + 1) * CHUNKS // 4) as chunk:
                    take_stats(chunk * STAT, chunk)
            aggregate(0)
            normalise(0, 0, 0)
            normalise(1, 0, 1)
            step(0, 1, 0, behind=0)
            dve.wait_ge(loaded[1], 32)
            step(1, 1, 1, 0, BANDS * BAND, behind=1)
            step(2, 2, 0, 1, BANDS * BAND)
            with dve.Fori(1, CHUNKS // 2) as i:
                two_steps(i, 2 * i, BANDS * BAND)
            for b in (1, 2):
                first = b * BANDS - 2
                two_steps(first, new_image=b)
                two_steps(first + 1)
                at = ((b + 1) % 2) * BANDS * BAND
                dve.wait_ge(loaded[b + 1], 32 * -(-2 * STAT // BAND))
                two_steps(first + 2, 0, at)
                dve.wait_ge(loaded[b + 1], 32 * BANDS)
                with dve.Fori(1, CHUNKS // 2) as n:
                    two_steps(n + (first + 2), 2 * n, at)
            two_steps((B - 1) * BANDS - 2, new_image=B - 1)
            with dve.Fori((B - 1) * BANDS - 1, GROUPS // 2 - 2) as i:
                two_steps(i)
            step(GROUPS - 3, B * BANDS - 1, 1)
            step(GROUPS - 2, None, 0, ahead=False)
            step(GROUPS - 1, None, 1, ahead=False)
            join(GROUPS - 2, 0, 1)
            for p in range(PAIRS):
                divide(GROUPS - 1, p)
            join(GROUPS - 1, 1, 0)
            join(GROUPS - 1, 1, 1)

        @block.tensor
        def _(pe):
            pe.wait_ge(w_loaded, 32)
            pe.wait_ge(consts, 8)
            for j in range(3):
                last = nc.tensor.transpose(psum[:, Q_BANK, j * C:(j + 1) * C], w_nat[:, j, :], ident[:, :])
            last.then_inc(w_transposed, 1)
            pe.wait_ge(w_ready, 1)

            def project_qk(g, par):
                pe.wait_ge(xn_ready, g + 1)
                wait(pe, pt_evac, 4 * (g - 2))
                nc.tensor.matmul(psum[:, K_BANK, 0:GT], w_t[:, 1, :], xn[:, par, :, 0:TOK], start=True, stop=True).then_inc(k_mm, 1)
                if isinstance(g, int):
                    wait(pe, q_evac, g)
                wait(pe, both_done, 2 * g - 5)
                nc.tensor.matmul(psum[:, Q_BANK, 0:GT], w_t[:, 0, :], xn[:, par, :, 0:TOK], start=True, stop=True).then_inc(q_mm, 1)

            def project_v(g, par):
                if isinstance(g, int):
                    wait(pe, v_evac, g)
                wait(pe, both_done, 2 * (g - 1))
                for p in range(PAIRS):
                    last = nc.tensor.matmul(psum[0:KROWS, V_BANK, p * C:(p + 1) * C],
                                            xn[:, par, 2 * p:2 * p + 2, :].rearrange("p w k -> p (w k)")[:, 0:KROWS],
                                            w_t[:, 2, :], start=True, stop=True, skip_group_check=True)
                last.then_inc(v_mm, 1)

            def scores(g, par, j):
                if j == 0:
                    pe.wait_ge(k_split, g + 1)
                    pe.wait_ge(q_split, g + 1)
                wait(pe, sub_done[1 - j], g + j)
                products = ((q_hi, k_hi), (q_hi, k_lo), (q_lo, k_hi))
                for w in range(GW):
                    for n, (q, k) in enumerate(products):
                        for h in (2 * j, 2 * j + 1):
                            rows = slice(h * PC, (h + 1) * PC)
                            last = nc.tensor.matmul(psum[:, h - 2 * j, w * TOK:(w + 1) * TOK], q[rows, par, w * ROWS2:w * ROWS2 + 128],
                                                    k[rows, par, w * TOK:(w + 1) * TOK], start=n == 0,
                                                    stop=n == len(products) - 1, skip_group_check=True)
                last.then_inc(s_mm[j], 1)

            def transpose_probs(c, par, p, ahead=True):
                if p == 0:
                    pe.wait_ge(exp_done[0], c + 1)
                    pe.wait_ge(exp_done[1], c + 1)
                    wait(pe, pt_evac, 4 * c - 1)
                elif p == 1:
                    if ahead:
                        pe.wait_ge(k_evac, c + 3)
                    else:
                        pe.wait_ge(pt_evac, 4 * c)
                else:
                    pe.wait_ge(pt_evac, 4 * c + p - 1)
                for h in range(HP):
                    last = nc.tensor.transpose(psum[0:KROWS, T_BANKS[p % 2], h * ROWS2:(h + 1) * ROWS2],
                                               probs[:, par, h, 2 * p:2 * p + 2, :].rearrange("p w k -> p (w k)")[:, 0:KROWS],
                                               ident[0:ROWS2, 0:ROWS2])
                last.then_inc(pt_mm, 1)

            def weighted_sum(c, par, p):
                pe.wait_ge(pt_evac, 4 * c + p + 1)
                pe.wait_ge(v_evac, c + 1)
                wait(pe, norm_done, 4 * c + p - 1)
                sums = psum[0:ROWS2, PV_BANKS[p % 2], 0:2 * HP * (PC + 1)].rearrange("p (w h d) -> p w h d", w=2, h=HP)
                for h in range(HP):
                    last = nc.tensor.matmul(sums[:, :, h, :], probs_t[:, p % 2, h, :], v_rows[:, par, p, h, :, :],
                                            start=True, stop=True, skip_group_check=True)
                last.then_inc(pv_mm, 1)

            def transpose_back(c, n, ahead=True):
                if n == 1:
                    wait(pe, v_evac, c + 2 if ahead else GROUPS)
                elif ahead:
                    pe.wait_ge(q_evac, c + 3)
                else:
                    pe.wait_ge(both_done, 2 * c - 1)
                pe.wait_ge(norm_done, 4 * c + 2 * (n + 1))
                for w in range(GW // 2):
                    last = nc.tensor.transpose(psum[:, BACK_BANKS[n], w * ROWS2:(w + 1) * ROWS2],
                                               mixed[:, 2 * n + w // 2, w % 2, :, :].rearrange("p h d -> p (h d)"),
                                               ident[0:ROWS2, 0:ROWS2])
                last.then_inc(back_mm, 1)

            def step(g, par, ahead=True, behind=2):
                scores(g, par, 0)
                if behind >= 2:
                    transpose_back(g - 2, 1)
                if ahead:
                    project_qk(g + 1, 1 - par)
                if behind:
                    transpose_probs(g - 1, 1 - par, 0)
                    transpose_probs(g - 1, 1 - par, 1, ahead)
                project_v(g, par)
                scores(g, par, 1)
                if behind:
                    weighted_sum(g - 1, 1 - par, 0)
                    transpose_probs(g - 1, 1 - par, 2)
                    weighted_sum(g - 1, 1 - par, 1)
                    transpose_probs(g - 1, 1 - par, 3)
                    weighted_sum(g - 1, 1 - par, 2)
                    weighted_sum(g - 1, 1 - par, 3)
                    transpose_back(g - 1, 0, ahead)

            project_qk(0, 0)
            step(0, 0, behind=0)
            step(1, 1, behind=1)
            step(2, 0)
            with pe.Fori(1, GROUPS // 2 - 1) as i:
                step(2 * i + 1, 1)
                step(2 * i + 2, 0)
            step(GROUPS - 1, 1, ahead=False)
            transpose_back(GROUPS - 2, 1)
            for p in range(PAIRS):
                transpose_probs(GROUPS - 1, 1, p, ahead=False)
                weighted_sum(GROUPS - 1, 1, p)
            transpose_back(GROUPS - 1, 0, ahead=False)
            transpose_back(GROUPS - 1, 1, ahead=False)


_INS = ["x", "L0_conv_w_qkv", "L0_conv_b_qkv"]
_OUT = (B, C, H, W)


def kernel(**inputs):
    import numpy as _np
    import concourse.bacc as _bacc
    from concourse.bass_utils import run_bass_kernel_spmd as _run

    nc = _bacc.Bacc("TRN2", target_bir_lowering=False, num_devices=1)
    arrays, args = {}, []
    for name in _INS:
        a = _np.ascontiguousarray(inputs[name])
        arrays[f"in_{name}_dram"] = a
        args.append(nc.dram_tensor(f"in_{name}_dram", a.shape, mybir.dt.from_np(a.dtype), kind="ExternalInput").ap())
    args.append(nc.dram_tensor("out_dram", _OUT, mybir.dt.float32, kind="ExternalOutput").ap())
    window_attention(nc, *args)
    r = _run(nc, [arrays], core_ids=[0])
    return r.results[0]["out_dram"]
```

```python
import numpy as np

import concourse.bass as bass
from concourse import mybir
from contextlib import ExitStack

B, C, H, W = 4, 128, 112, 112
WS, SHIFT, HEADS, GN_GROUPS = 7, 3, 8, 32
HD = C // HEADS
PER = C // GN_GROUPS
EPS = 1e-5
TOK = WS * WS
BANDS = H // WS
NW = W // WS
GW = NW // 2
GT = GW * TOK
PAIRS = GW // 2
HP = HEADS // 2
PC = 2 * HD
ROWS2 = 2 * TOK
PITCH = 64
KROWS = PITCH + TOK
BAND = WS * W
SLOTS = 2 * BANDS
GROUPS = B * BANDS * 2
STAT = 448
CHUNKS = H * W // STAT
Q_LEN = GW * ROWS2
Q_PAD = 128 - ROWS2
NEWTON = 4
AGG = 14 + 4 * NEWTON
X_SCALE, W_SCALE = 8.0, 256.0
QK_SCALE = 1.0 / 16


def window_attention(nc, x, w_qkv, b_qkv, out):
    f32, f16, i32 = mybir.dt.float32, mybir.dt.float16, mybir.dt.int32
    ALU, ACT, AX = mybir.AluOpType, mybir.ActivationFunctionType, mybir.AxisListType

    x_v = x.rearrange("b c h w -> b c (h w)")
    out_v = out.rearrange("b c h w -> b c (h w)")

    ctx = ExitStack()
    with ctx:
        def sb(name, shape, dt=f32):
            return ctx.enter_context(nc.sbuf_tensor(name, shape, dt))

        def sem(name):
            return ctx.enter_context(nc.semaphore(name))

        image = sb("image", [C, SLOTS * BAND])
        xn = sb("xn", [C, GW, TOK])
        xn_hi, xn_lo = sb("xn_hi", [C, 2, GW, PITCH], f16), sb("xn_lo", [C, 2, GW, PITCH], f16)
        k32 = sb("k32", [C, GT])
        q32 = sb("q32", [C, GW, 2, TOK])
        k_hi, k_lo = sb("k_hi", [C, 2, GT], f16), sb("k_lo", [C, 2, GT], f16)
        q_hi, q_lo = sb("q_hi", [C, 2, Q_LEN + Q_PAD], f16), sb("q_lo", [C, 2, Q_LEN + Q_PAD], f16)
        row_max = sb("row_max", [ROWS2, 2, 2, GW])
        shifted = sb("shifted", [ROWS2, 2, 2, GW, TOK])
        probs = sb("probs", [ROWS2, 2, HP, GW, PITCH])
        probs_t = sb("probs_t", [KROWS, 2, HP, ROWS2])
        v_rows = sb("v_rows", [KROWS, 2, PAIRS, HP, 2, PC + 1])
        inv_sum = sb("inv_sum", [ROWS2, 2, 2, HP * 2])
        mixed = sb("mixed", [ROWS2, PAIRS, 2, HP, PC])
        even_out = sb("even_out", [C, 2, GW // 2, TOK])
        both_out = sb("both_out", [C, 2, GW, TOK])
        stage = sb("stage", [C, 2 * BAND])
        w_nat = sb("w_nat", [C, 3, C])
        w_t = sb("w_t", [C, 3, C])
        w_hi, w_lo = sb("w_hi", [C, 3, C], f16), sb("w_lo", [C, 3, C], f16)
        bias = sb("bias", [C, 3])
        ident = sb("ident", [C, C])
        head_of = sb("head_of", [C, HEADS])
        even_odd = sb("even_odd", [C, 2])
        size = sb("size", [C, 3])
        size_b = sb("size_b", [C, 3])
        size_all = sb("size_all", [C, 3])
        fit = sb("fit", [C, 3])
        qk_fit = sb("qk_fit", [C, 2])
        q_scale, q_bias = sb("q_scale", [C, 2]), sb("q_bias", [C, 2])
        v_scale = sb("v_scale", [C, 2])
        k_bias = sb("k_bias", [C, 1])
        exp_scale = sb("exp_scale", [C, 1])
        stats = sb("stats", [C, CHUNKS, 6])
        mean_blk, var_blk = sb("mean_blk", [C, 32]), sb("var_blk", [C, 32])
        mean_row, var_row = sb("mean_row", [C, 32]), sb("var_row", [C, 32])
        work_a, work_b = sb("work_a", [C, 32]), sb("work_b", [C, 32])
        g_mean, g_var, rs, rs_t = (sb(n, [C, 8]) for n in ("g_mean", "g_var", "rs", "rs_t"))
        half_bits = sb("half_bits", [C, 8], i32)
        agg = sb("agg", [C, 2])
        mean_c, rstd_c = sb("mean_c", [C, 32]), sb("rstd_c", [C, 32])

        psum = ctx.enter_context(nc.psum_tensor("psum", [128, 8, 512], f32))
        S_BANKS, T_BANKS, PV_BANKS = slice(0, 2), (3, 2), slice(4, 6)
        K_BANK, Q_BANK, V_BANK, BACK_BANKS = 2, 6, 7, (6, 7)

        loaded0 = [sem(f"loaded_first_{n}") for n in range(4)]
        loaded = [None] + [sem(f"loaded_image_{b}") for b in range(1, B)]
        w_loaded, stored = sem("w_loaded"), sem("stored")
        consts, sized, w_transposed, ready = (sem(n) for n in ("consts", "sized", "w_transposed", "ready"))
        pool_chain, dve_chain, agg_chain = sem("pool_chain"), sem("dve_chain"), sem("agg_chain")
        stats_done, waited, waited_sp = sem("stats_done"), sem("waited"), sem("waited_sp")
        x_high, x_split = sem("x_high"), sem("x_split")
        xn_ready, q_mm, k_mm, v_mm = sem("xn_ready"), sem("q_mm"), sem("k_mm"), sem("v_mm")
        q_evac, k_evac, v_evac = sem("q_evac"), sem("k_evac"), sem("v_evac")
        k_high, q_high, k_split, q_split = sem("k_high"), sem("q_high"), sem("k_split"), sem("q_split")
        s_mm = [sem("s_mm_0"), sem("s_mm_1")]
        max_done = [sem("max_done_0"), sem("max_done_1")]
        sub_done = [sem("sub_done_0"), sem("sub_done_1")]
        exp_done = [sem("exp_done_0"), sem("exp_done_1")]
        pt_mm, pt_evac, pv_mm = sem("pt_mm"), sem("pt_evac"), sem("pv_mm")
        inv_done, norm_done = sem("inv_done"), sem("norm_done")
        back_mm, even_done, both_done, add_done = sem("back_mm"), sem("even_done"), sem("both_done"), sem("add_done")

        def wait(engine, semaphore, count):
            if not isinstance(count, int) or count > 0:
                engine.wait_ge(semaphore, count)

        def in_windows(flat, first, n):
            rows = flat.rearrange("p (r c) -> p r c", c=W)[:, :, first:first + n * WS]
            return rows.rearrange("p r (w c) -> p w r c", c=WS)

        def pieces(half):
            if half == 0:
                return [(0, GW, 0, WS, SHIFT)]
            first = SHIFT + GW * WS
            return [(0, GW - 1, 0, WS, first), (GW - 1, 1, 0, WS - SHIFT, W - (WS - SHIFT)), (GW - 1, 1, WS - SHIFT, SHIFT, 0)]

        def token_view(tokens, piece):
            w0, n, c0, nc_, _ = piece
            return tokens[:, w0:w0 + n, :].rearrange("p w (r c) -> p w r c", c=WS)[:, :, :, c0:c0 + nc_]

        def pixel_view(flat, piece):
            w0, n, c0, nc_, first = piece
            if n > 1:
                return in_windows(flat, first, n)
            rows = flat.rearrange("p (r c) -> p r c", c=W)[:, :, first:first + nc_]
            return rows.rearrange("p r (w c) -> p w r c", c=nc_)

        block = ctx.enter_context(nc.Block())

        @block.sync
        def _(sp):
            sp.dma_start(w_nat[:, :, :], w_qkv.rearrange("(j o) c -> o j c", j=3)).then_inc(w_loaded, 16)
            sp.dma_start(bias[:, :], b_qkv.rearrange("(j o) -> o j", j=3), allow_slow_non_contiguous=True).then_inc(w_loaded, 16)

            def load_rows(b, row, n, semaphore, slot_row):
                sp.dma_start(image[:, slot_row * W:(slot_row + n) * W],
                             x_v[b, :, row * W:(row + n) * W]).then_inc(semaphore, 16)

            quarter = H // 4
            for n in range(3):
                load_rows(0, n * quarter + SHIFT, quarter, loaded0[n], n * quarter)
            load_rows(0, 3 * quarter + SHIFT, quarter - SHIFT, loaded0[3], 3 * quarter)
            load_rows(0, 0, SHIFT, loaded0[3], H - SHIFT)
            load_rows(1, SHIFT, H - SHIFT, loaded[1], H)
            load_rows(1, 0, SHIFT, loaded[1], 2 * H - SHIFT)

            def store_band(b, y):
                t = b * BANDS + y
                sp.wait_ge(add_done, 2 * t + 2)
                sp.sem_inc(waited_sp, 1)
                at = (y & 1) * BAND
                top = (WS - SHIFT) * W
                src = stage[:, bass.ds(at, BAND)]
                sp.dma_start(out_v[bass.ds(b, 1), :, bass.ds((y * WS + SHIFT) * W, top)].rearrange("b c n -> c (b n)"),
                             src[:, 0:top]).then_inc(stored, 16)
                sp.dma_start(out_v[bass.ds(b, 1), :, bass.ds(((y + 1) & (BANDS - 1)) * BAND, BAND - top)]
                             .rearrange("b c n -> c (b n)"), src[:, top:BAND]).then_inc(stored, 16)

            def load_band(b_static, y):
                at = (b_static % 2) * BANDS * BAND + y * BAND
                top = (WS - SHIFT) * W
                slot = image[:, bass.ds(at, BAND)]
                sp.dma_start(slot[:, 0:top], x_v[b_static, :, bass.ds((y * WS + SHIFT) * W, top)]).then_inc(loaded[b_static], 16)
                sp.dma_start(slot[:, top:BAND], x_v[b_static, :, bass.ds(((y + 1) & (BANDS - 1)) * BAND, BAND - top)]
                             ).then_inc(loaded[b_static], 16)

            def wait_stored(b, y):
                sp.wait_ge(stored, 32 * (b * BANDS + y) + 32)
                sp.sem_inc(waited_sp, 1)

            for b in range(2):
                with sp.Fori(0, BANDS) as y:
                    store_band(b, y)
                    load_band(b + 2, y)
                    sp.wait_ge(loaded[b + 2], 32 * y + 32)
                    wait_stored(b, y)
            with sp.Fori(2, B) as b:
                with sp.Fori(0, BANDS) as y:
                    store_band(b, y)
                    wait_stored(b, y)

        @block.gpsimd
        def _(pool):
            nc.gpsimd.memset(ident[:, :], 0.0).then_inc(pool_chain, 1)
            nc.gpsimd.memset(head_of[:, :], 1.0).then_inc(pool_chain, 1)
            pool.wait_ge(pool_chain, 2)
            nc.gpsimd.affine_select(out=ident[:, :], in_=ident[:, :], compare_op=ALU.not_equal, fill=1.0, base=0,
                                    pattern=[[-1, C]], channel_multiplier=1).then_inc(consts, 1)
            nc.gpsimd.affine_select(out=head_of[:, :], in_=head_of[:, :], compare_op=ALU.is_ge, fill=0.0, base=0,
                                    pattern=[[-HD, HEADS]], channel_multiplier=1).then_inc(pool_chain, 1)
            pool.wait_ge(pool_chain, 3)
            nc.gpsimd.affine_select(out=head_of[:, :], in_=head_of[:, :], compare_op=ALU.is_ge, fill=0.0, base=HD - 1,
                                    pattern=[[HD, HEADS]], channel_multiplier=-1).then_inc(consts, 1)
            nc.gpsimd.memset(probs[:, :, :, :, TOK:PITCH], 0.0).then_inc(consts, 1)
            nc.gpsimd.memset(q_hi[:, :, Q_LEN:], 0.0).then_inc(consts, 1)
            nc.gpsimd.memset(q_lo[:, :, Q_LEN:], 0.0).then_inc(consts, 1)
            nc.gpsimd.memset(v_rows[:, :, :, :, :, :], 0.0).then_inc(pool_chain, 1)
            pool.wait_ge(pool_chain, 4)
            nc.gpsimd.memset(v_rows[0:TOK, :, :, :, 0, PC:PC + 1], 1.0).then_inc(consts, 1)
            nc.gpsimd.memset(v_rows[PITCH:KROWS, :, :, :, 1, PC:PC + 1], 1.0).then_inc(consts, 1)
            pool.wait_ge(sized, 1)
            pool.wait_ge(consts, 7)
            nc.gpsimd.partition_all_reduce(size_all[:, :], size[:, :], C, bass.bass_isa.ReduceOp.max).then_inc(consts, 1)

            def split_x(g, par):
                wait(pool, v_mm, g - 1)
                pool.wait_ge(xn_ready, g + 1)
                pool.sem_inc(waited, 1)
                nc.gpsimd.tensor_scalar(xn_hi[:, par, :, 0:TOK], xn[:, :, :], 1.0, 0.0, ALU.mult, ALU.add).then_inc(x_high, 1)
                pool.wait_ge(x_high, g + 1)
                nc.gpsimd.tensor_tensor(xn_lo[:, par, :, 0:TOK], xn[:, :, :], xn_hi[:, par, :, 0:TOK],
                                        ALU.subtract).then_inc(x_split, 1)

            def split(g, par):
                pool.wait_ge(k_evac, g + 1)
                wait(pool, s_mm[1], g - 1)
                pool.sem_inc(waited, 1)
                nc.gpsimd.tensor_scalar(k_hi[:, par, :], k32[:, :], 1.0, 0.0, ALU.mult, ALU.add).then_inc(k_high, 1)
                pool.wait_ge(k_high, g + 1)
                nc.gpsimd.tensor_tensor(k_lo[:, par, :], k32[:, :], k_hi[:, par, :], ALU.subtract).then_inc(k_split, 1)
                pool.wait_ge(q_evac, g + 1)
                q_flat = q32[:, :, :, :].rearrange("p w e q -> p (w e q)")
                pool.sem_inc(waited, 1)
                nc.gpsimd.tensor_scalar(q_hi[:, par, 0:Q_LEN], q_flat, 1.0, 0.0, ALU.mult, ALU.add).then_inc(q_high, 1)
                pool.wait_ge(q_high, g + 1)
                nc.gpsimd.tensor_tensor(q_lo[:, par, 0:Q_LEN], q_flat, q_hi[:, par, 0:Q_LEN], ALU.subtract).then_inc(q_split, 1)

            def add_image(g, t, half):
                pool.wait_ge(both_done, 2 * g + 2)
                if half == 0:
                    wait(pool, stored, 32 * (t - 1))
                at, st = (t & (SLOTS - 1)) * BAND, (t & 1) * BAND
                for piece in pieces(half):
                    last = nc.gpsimd.tensor_tensor(pixel_view(stage[:, bass.ds(st, BAND)], piece), token_view(both_out[:, half], piece),
                                                   pixel_view(image[:, bass.ds(at, BAND)], piece), ALU.add)
                last.then_inc(add_done, 1)

            split_x(0, 0)
            split_x(1, 1)
            split(0, 0)
            split(1, 1)
            split_x(2, 0)
            split(2, 0)
            split_x(3, 1)

            def two_steps(i):
                split(2 * i + 3, 1)
                split_x(2 * i + 4, 0)
                add_image(2 * i, i, 0)
                split(2 * i + 4, 0)
                split_x(2 * i + 5, 1)
                add_image(2 * i + 1, i, 1)

            two_steps(0)
            two_steps(1)
            with pool.Fori(2, GROUPS // 2 - 2) as i:
                two_steps(i)
            split(GROUPS - 1, 1)
            for g in range(GROUPS - 4, GROUPS):
                add_image(g, g // 2, g % 2)

        @block.scalar
        def _(act):
            act.wait_ge(ready, 1)

            def evac_qk(g):
                act.wait_ge(k_mm, g + 1)
                wait(act, k_split, g)
                nc.scalar.activation(k32[:, :], psum[:, K_BANK, 0:GT], ACT.Identity, bias=k_bias[:, 0:1],
                                     scale=QK_SCALE).then_inc(k_evac, 1)
                act.wait_ge(q_mm, g + 1)
                wait(act, q_split, g)
                q = psum[:, Q_BANK, 0:GT].rearrange("p (w q) -> p w q", q=TOK)
                for e in range(2):
                    last = nc.scalar.activation(q32[:, :, e, :], q, ACT.Identity, bias=q_bias[:, e:e + 1],
                                                scale=q_scale[:, e:e + 1])
                last.then_inc(q_evac, 1)

            def evac_probs_t(c, p):
                act.wait_ge(pt_mm, 4 * c + p + 1)
                wait(act, pv_mm, 4 * c + p - 1)
                nc.scalar.copy(probs_t[:, p % 2, :, :], psum[0:KROWS, T_BANKS[p % 2], 0:HP * ROWS2]
                               .rearrange("p (h q) -> p h q", h=HP)).then_inc(pt_evac, 1)

            def evac_v(g, par):
                act.wait_ge(v_mm, g + 1)
                wait(act, pv_mm, 4 * (g - 1))
                v = psum[:, V_BANK, :].rearrange("p (a h d) -> p a h d", a=PAIRS, h=HP)
                nc.scalar.copy(v_rows[0:TOK, par, :, :, 0, 0:PC], v[0:TOK])
                nc.scalar.copy(v_rows[PITCH:KROWS, par, :, :, 1, 0:PC], v[PITCH:KROWS]).then_inc(v_evac, 1)

            def exp(g, par, j):
                act.wait_ge(sub_done[j], g + 1)
                wait(act, pt_mm, 4 * (g - 1))
                nc.scalar.activation(probs[:, par, 2 * j:2 * j + 2, :, 0:TOK], shifted[:, j, :, :, :], ACT.Exp,
                                     scale=exp_scale[0:ROWS2, 0:1]).then_inc(exp_done[j], 1)

            def evac_back(c, n):
                act.wait_ge(back_mm, 2 * c + n + 1)
                wait(act, both_done, 2 * c + n - 1)
                back = psum[:, BACK_BANKS[n], 0:GW // 2 * ROWS2].rearrange("p (w e q) -> p w e q", e=2, q=TOK)
                nc.scalar.activation(even_out[:, n, :, :], back[:, :, 0, :], ACT.Identity, bias=bias[:, 2:3],
                                     scale=v_scale[:, 0:1]).then_inc(even_done, 1)

            def step(g, par, ahead=True, behind=2):
                if ahead:
                    evac_qk(g + 1)
                evac_v(g, par)
                if behind:
                    evac_probs_t(g - 1, 0)
                    evac_probs_t(g - 1, 1)
                if behind >= 2:
                    evac_back(g - 2, 0)
                    evac_back(g - 2, 1)
                exp(g, par, 0)
                if behind:
                    evac_probs_t(g - 1, 2)
                    evac_probs_t(g - 1, 3)
                exp(g, par, 1)

            evac_qk(0)
            step(0, 0, behind=0)
            step(1, 1, behind=1)
            step(2, 0)
            with act.Fori(1, GROUPS // 2 - 1) as i:
                step(2 * i + 1, 1)
                step(2 * i + 2, 0)
            step(GROUPS - 1, 1, ahead=False)
            evac_probs_t(GROUPS - 1, 0)
            evac_probs_t(GROUPS - 1, 1)
            evac_back(GROUPS - 2, 0)
            evac_back(GROUPS - 2, 1)
            evac_probs_t(GROUPS - 1, 2)
            evac_probs_t(GROUPS - 1, 3)
            evac_back(GROUPS - 1, 0)
            evac_back(GROUPS - 1, 1)

        @block.vector
        def _(dve):
            chained = [0]

            def chain(instruction):
                chained[0] += 1
                instruction.then_inc(dve_chain, 1)
                dve.wait_ge(dve_chain, chained[0])

            chain(nc.vector.memset(mean_blk[:, :], 0.0))
            chain(nc.vector.memset(var_blk[:, :], 0.0))
            chain(nc.vector.memset(xn_hi[:, :, :, TOK:PITCH], 0.0))
            chain(nc.vector.memset(xn_lo[:, :, :, TOK:PITCH], 0.0))
            dve.wait_ge(w_loaded, 32)
            chain(nc.vector.tensor_reduce(size[:, :], w_nat[:, :, :], AX.X, ALU.add, apply_absolute_value=True))
            chain(nc.vector.tensor_reduce(size_b[:, :], bias[:, :].rearrange("p (j o) -> p j o", o=1), AX.X, ALU.add,
                                          apply_absolute_value=True))
            nc.vector.tensor_tensor(size[:, :], size[:, :], size_b[:, :], ALU.add).then_inc(sized, 1)
            dve.wait_ge(consts, 8)
            chain(nc.vector.tensor_reduce(even_odd[:, :], head_of[:, :].rearrange("p (h e) -> p e h", e=2), AX.X, ALU.add))
            chain(nc.vector.tensor_scalar(size_all[:, :], size_all[:, :], 1e-12, 1.0 / W_SCALE, ALU.max, ALU.mult))
            chain(nc.vector.reciprocal(fit[:, :], size_all[:, :]))
            chain(nc.vector.tensor_scalar(qk_fit[:, :], fit[:, 0:2], X_SCALE * QK_SCALE, None, ALU.mult))
            chain(nc.vector.tensor_scalar(q_scale[:, :], even_odd[:, :], QK_SCALE, None, ALU.mult))
            chain(nc.vector.tensor_scalar(q_bias[:, :], even_odd[:, :], bias[:, 0:1], qk_fit[:, 0:1], ALU.mult, ALU.mult))
            chain(nc.vector.tensor_scalar(k_bias[:, :], qk_fit[:, 1:2], bias[:, 1:2], None, ALU.mult))
            chain(nc.vector.tensor_scalar(v_scale[:, :], even_odd[:, :], size_all[:, 2:3], 1.0 / X_SCALE, ALU.mult, ALU.mult))
            chain(nc.vector.tensor_scalar(exp_scale[:, :], size_all[:, 0:1], size_all[:, 1:2], None, ALU.mult))
            chain(nc.vector.tensor_scalar(exp_scale[:, :], exp_scale[:, :], float(HD) ** -0.5 / (X_SCALE * QK_SCALE) ** 2, None,
                                          ALU.mult))
            dve.wait_ge(w_transposed, 1)
            for n in range(3):
                chain(nc.vector.tensor_scalar(w_t[:, n, :], psum[:, Q_BANK, n * C:(n + 1) * C], fit[:, n:n + 1], None, ALU.mult))
            chain(nc.vector.tensor_copy(w_hi[:, :, :], w_t[:, :, :]))
            nc.vector.tensor_tensor(w_lo[:, :, :], w_t[:, :, :], w_hi[:, :, :], ALU.subtract).then_inc(ready, 1)

            def take_stats(at, chunk):
                nc.vector.bn_stats(stats[:, bass.ds(chunk, 1), :].rearrange("p o s -> p (o s)"),
                                   image[:, bass.ds(at, STAT)]).then_inc(stats_done, 1)

            def aggregate(b):
                links = [0]

                def link(instruction):
                    links[0] += 1
                    instruction.then_inc(agg_chain, 1)
                    dve.wait_ge(agg_chain, b * AGG + links[0])

                def grouped(rows):
                    return rows[:, :].rearrange("p (g c) -> p g c", c=PER)

                dve.wait_ge(stats_done, CHUNKS * (b + 1))
                link(nc.vector.bn_aggr(agg[:, :], stats[:, :, :].rearrange("p n s -> p (n s)")))
                nc.vector.tensor_copy(mean_blk[:, 0:1], agg[:, 0:1])
                link(nc.vector.tensor_copy(var_blk[:, 0:1], agg[:, 1:2]))
                nc.vector.transpose(mean_row[:, :], mean_blk[:, :])
                link(nc.vector.transpose(var_row[:, :], var_blk[:, :]))
                link(nc.vector.tensor_reduce(g_mean[:, :], grouped(mean_row), AX.X, ALU.add))
                link(nc.vector.tensor_scalar(g_mean[:, :], g_mean[:, :], 1.0 / PER, None, ALU.mult))
                link(nc.vector.tensor_tensor(grouped(work_a), grouped(mean_row),
                                             g_mean[:, :, None].broadcast_to([C, 8, PER]), ALU.subtract))
                link(nc.vector.tensor_tensor(work_b[:, :], work_a[:, :], work_a[:, :], ALU.mult))
                link(nc.vector.tensor_tensor(work_a[:, :], work_b[:, :], var_row[:, :], ALU.add))
                link(nc.vector.tensor_reduce(g_var[:, :], grouped(work_a), AX.X, ALU.add))
                link(nc.vector.tensor_scalar(g_var[:, :], g_var[:, :], 1.0 / PER, EPS, ALU.mult, ALU.add))
                link(nc.vector.tensor_scalar(half_bits[:, :], g_var[:, :].bitcast(i32), 1, None, ALU.logical_shift_right))
                link(nc.vector.tensor_scalar(rs[:, :].bitcast(i32), half_bits[:, :], -1.0, float(0x5F3759DF), ALU.mult, ALU.add))
                for _ in range(NEWTON):
                    link(nc.vector.tensor_tensor(rs_t[:, :], rs[:, :], rs[:, :], ALU.mult))
                    link(nc.vector.tensor_tensor(rs_t[:, :], rs_t[:, :], g_var[:, :], ALU.mult))
                    link(nc.vector.tensor_scalar(rs_t[:, :], rs_t[:, :], -0.5, 1.5, ALU.mult, ALU.add))
                    link(nc.vector.tensor_tensor(rs[:, :], rs[:, :], rs_t[:, :], ALU.mult))
                nc.vector.tensor_copy(grouped(mean_row), g_mean[:, :, None].broadcast_to([C, 8, PER]))
                link(nc.vector.tensor_scalar(grouped(var_row), rs[:, :, None].broadcast_to([C, 8, PER]), X_SCALE, None, ALU.mult))
                nc.vector.transpose(mean_c[:, :], mean_row[:, :])
                link(nc.vector.transpose(rstd_c[:, :], var_row[:, :]))
                assert links[0] == AGG

            def normalise(g, t, half):
                wait(dve, x_split, g)
                at = (t & (SLOTS - 1)) * BAND
                for piece in pieces(half):
                    last = nc.vector.tensor_scalar(token_view(xn, piece),
                                                   pixel_view(image[:, bass.ds(at, BAND)], piece),
                                                   mean_c[:, 0:1], rstd_c[:, 0:1], ALU.subtract, ALU.mult)
                last.then_inc(xn_ready, 1)

            def maximum(g, j):
                dve.wait_ge(s_mm[j], g + 1)
                nc.vector.tensor_reduce(row_max[:, j, :, :], psum[0:ROWS2, S_BANKS, 0:GT]
                                        .rearrange("p h (w k) -> p h w k", k=TOK), AX.X, ALU.max).then_inc(max_done[j], 1)

            def subtract(g, j):
                dve.wait_ge(max_done[j], g + 1)
                wait(dve, exp_done[j], g)
                nc.vector.tensor_tensor(shifted[:, j, :, :, :], psum[0:ROWS2, S_BANKS, 0:GT]
                                        .rearrange("p h (w k) -> p h w k", k=TOK),
                                        row_max[:, j, :, :, None].broadcast_to([ROWS2, 2, GW, TOK]),
                                        ALU.subtract).then_inc(sub_done[j], 1)

            def divide(c, n):
                rows = psum[0:ROWS2, PV_BANKS, 0:HP * 2 * (PC + 1)].rearrange("p a (n d) -> p a n d", d=PC + 1)
                dve.wait_ge(pv_mm, 4 * c + 2 * n + 2)
                nc.vector.reciprocal(inv_sum[:, n, :, :], rows[:, :, :, PC]).then_inc(inv_done, 1)
                dve.wait_ge(inv_done, 2 * c + n + 1)
                wait(dve, back_mm, 2 * (c - 1) + n + 1)
                nc.vector.tensor_tensor(mixed[:, 2 * n:2 * n + 2, :, :, :].rearrange("p a w h d -> p a (w h) d"), rows[:, :, :, 0:PC],
                                        inv_sum[:, n, :, :, None].broadcast_to([ROWS2, 2, HP * 2, PC]), ALU.mult).then_inc(norm_done, 1)

            def join(c, par, n):
                dve.wait_ge(even_done, 2 * c + n + 1)
                wait(dve, add_done, c - 1)
                back = psum[:, BACK_BANKS[n], 0:GW // 2 * ROWS2].rearrange("p (w e q) -> p w e q", e=2, q=TOK)
                nc.vector.scalar_tensor_tensor(both_out[:, par, GW // 2 * n:GW // 2 * (n + 1), :], back[:, :, 1, :],
                                               v_scale[:, 1:2], even_out[:, n, :, :], ALU.mult, ALU.add).then_inc(both_done, 1)

            def step(g, t2, par, chunk=None, image_at=None, ahead=True, behind=2):
                maximum(g, 0)
                subtract(g, 0)
                if behind >= 2:
                    divide(g - 2, 1)
                if chunk is not None:
                    take_stats(image_at + chunk * STAT, chunk)
                if ahead:
                    normalise(g + 2, t2, par)
                maximum(g, 1)
                subtract(g, 1)
                if behind >= 2:
                    join(g - 2, par, 0)
                    join(g - 2, par, 1)
                if behind:
                    divide(g - 1, 0)

            def two_steps(i, chunk=None, image_at=None, new_image=None):
                step(2 * i + 1, i + 1, 1, chunk, image_at)
                if new_image is not None:
                    aggregate(new_image)
                step(2 * i + 2, i + 2, 0, None if chunk is None else chunk + 1, image_at)

            for n in range(4):
                dve.wait_ge(loaded0[n], 16 if n < 3 else 32)
                with dve.Fori(n * CHUNKS // 4, (n + 1) * CHUNKS // 4) as chunk:
                    take_stats(chunk * STAT, chunk)
            aggregate(0)
            normalise(0, 0, 0)
            normalise(1, 0, 1)
            step(0, 1, 0, behind=0)
            dve.wait_ge(loaded[1], 32)
            step(1, 1, 1, 0, BANDS * BAND, behind=1)
            step(2, 2, 0, 1, BANDS * BAND)
            two_steps(1, 2, BANDS * BAND)
            with dve.Fori(2, CHUNKS // 2) as i:
                two_steps(i, 2 * i, BANDS * BAND)
            for b in (1, 2):
                first = b * BANDS - 2
                two_steps(first, new_image=b)
                two_steps(first + 1)
                at = ((b + 1) % 2) * BANDS * BAND
                dve.wait_ge(loaded[b + 1], 32 * -(-2 * STAT // BAND))
                two_steps(first + 2, 0, at)
                dve.wait_ge(loaded[b + 1], 32 * BANDS)
                with dve.Fori(1, CHUNKS // 2) as n:
                    two_steps(n + (first + 2), 2 * n, at)
            two_steps((B - 1) * BANDS - 2, new_image=B - 1)
            with dve.Fori((B - 1) * BANDS - 1, GROUPS // 2 - 2) as i:
                two_steps(i)
            step(GROUPS - 3, B * BANDS - 1, 1)
            step(GROUPS - 2, None, 0, ahead=False)
            step(GROUPS - 1, None, 1, ahead=False)
            divide(GROUPS - 2, 1)
            join(GROUPS - 2, 0, 0)
            join(GROUPS - 2, 0, 1)
            divide(GROUPS - 1, 0)
            divide(GROUPS - 1, 1)
            join(GROUPS - 1, 1, 0)
            join(GROUPS - 1, 1, 1)

        @block.tensor
        def _(pe):
            pe.wait_ge(w_loaded, 32)
            pe.wait_ge(consts, 8)
            for j in range(3):
                last = nc.tensor.transpose(psum[:, Q_BANK, j * C:(j + 1) * C], w_nat[:, j, :], ident[:, :])
            last.then_inc(w_transposed, 1)
            pe.wait_ge(ready, 1)

            products = ((w_hi, xn_hi), (w_hi, xn_lo), (w_lo, xn_hi))

            def project_qk(g, par):
                pe.wait_ge(x_split, g + 1)
                wait(pe, pt_evac, 4 * (g - 2))
                for n, (w, xs) in enumerate(products):
                    last = nc.tensor.matmul(psum[:, K_BANK, 0:GT], w[:, 1, :], xs[:, par, :, 0:TOK], start=n == 0, stop=n == 2)
                last.then_inc(k_mm, 1)
                if isinstance(g, int):
                    wait(pe, q_evac, g)
                wait(pe, both_done, 2 * (g - 4) + 1)
                for n, (w, xs) in enumerate(products):
                    last = nc.tensor.matmul(psum[:, Q_BANK, 0:GT], w[:, 0, :], xs[:, par, :, 0:TOK], start=n == 0, stop=n == 2)
                last.then_inc(q_mm, 1)

            def project_v(g, par):
                if isinstance(g, int):
                    wait(pe, v_evac, g)
                wait(pe, both_done, 2 * (g - 3) + 2)
                for p in range(PAIRS):
                    for n, (w, xs) in enumerate(products):
                        last = nc.tensor.matmul(psum[:, V_BANK, p * C:(p + 1) * C],
                                                xs[:, par, 2 * p:2 * p + 2, :].rearrange("p w k -> p (w k)"),
                                                w[:, 2, :], start=n == 0, stop=n == 2, skip_group_check=True)
                last.then_inc(v_mm, 1)

            def scores(g, par, j):
                if j == 0:
                    pe.wait_ge(k_split, g + 1)
                    pe.wait_ge(q_split, g + 1)
                wait(pe, sub_done[1 - j], g + j)
                for w in range(GW):
                    for n, (q, k) in enumerate(((q_hi, k_hi), (q_hi, k_lo), (q_lo, k_hi))):
                        for h in (2 * j, 2 * j + 1):
                            rows = slice(h * PC, (h + 1) * PC)
                            last = nc.tensor.matmul(psum[:, h - 2 * j, w * TOK:(w + 1) * TOK], q[rows, par, w * ROWS2:w * ROWS2 + 128],
                                                    k[rows, par, w * TOK:(w + 1) * TOK], start=n == 0,
                                                    stop=n == 2, skip_group_check=True)
                last.then_inc(s_mm[j], 1)

            def transpose_probs(c, par, p, ahead=True):
                if p == 0:
                    pe.wait_ge(exp_done[0], c + 1)
                    pe.wait_ge(exp_done[1], c + 1)
                    wait(pe, pt_evac, 4 * c - 1)
                elif p == 1:
                    if ahead:
                        pe.wait_ge(k_evac, c + 3)
                    else:
                        pe.wait_ge(pt_evac, 4 * c)
                else:
                    pe.wait_ge(pt_evac, 4 * c + p - 1)
                for h in range(HP):
                    last = nc.tensor.transpose(psum[0:KROWS, T_BANKS[p % 2], h * ROWS2:(h + 1) * ROWS2],
                                               probs[:, par, h, 2 * p:2 * p + 2, :].rearrange("p w k -> p (w k)")[:, 0:KROWS],
                                               ident[0:ROWS2, 0:ROWS2])
                last.then_inc(pt_mm, 1)

            def weighted_sum(c, par, p):
                pe.wait_ge(pt_evac, 4 * c + p + 1)
                pe.wait_ge(v_evac, c + 1)
                wait(pe, norm_done, 2 * c + p // 2)
                sums = psum[0:ROWS2, PV_BANKS.start + p % 2, 0:2 * HP * (PC + 1)].rearrange("p (w h d) -> p w h d", w=2, h=HP)
                for h in range(HP):
                    last = nc.tensor.matmul(sums[:, :, h, :], probs_t[:, p % 2, h, :], v_rows[:, par, p, h, :, :],
                                            start=True, stop=True, skip_group_check=True)
                last.then_inc(pv_mm, 1)

            def transpose_back(c, n, projected=True):
                if not projected:
                    pe.wait_ge(both_done, 2 * c + n - 1)
                elif n == 0:
                    pe.wait_ge(q_evac, c + 4)
                else:
                    pe.wait_ge(v_evac, c + 3)
                pe.wait_ge(norm_done, 2 * c + n + 1)
                for w in range(GW // 2):
                    last = nc.tensor.transpose(psum[:, BACK_BANKS[n], w * ROWS2:(w + 1) * ROWS2],
                                               mixed[:, 2 * n + w // 2, w % 2, :, :].rearrange("p h d -> p (h d)"),
                                               ident[0:ROWS2, 0:ROWS2])
                last.then_inc(back_mm, 1)

            def step(g, par, ahead=True, behind=2):
                scores(g, par, 0)
                if behind >= 2:
                    weighted_sum(g - 2, par, 2)
                    weighted_sum(g - 2, par, 3)
                if ahead:
                    project_qk(g + 1, 1 - par)
                project_v(g, par)
                if behind:
                    transpose_probs(g - 1, 1 - par, 0)
                    transpose_probs(g - 1, 1 - par, 1, ahead)
                scores(g, par, 1)
                if behind >= 2:
                    transpose_back(g - 2, 0, ahead)
                    transpose_back(g - 2, 1)
                if behind:
                    weighted_sum(g - 1, 1 - par, 0)
                    weighted_sum(g - 1, 1 - par, 1)
                    transpose_probs(g - 1, 1 - par, 2)
                    transpose_probs(g - 1, 1 - par, 3)

            project_qk(0, 0)
            step(0, 0, behind=0)
            step(1, 1, behind=1)
            step(2, 0)
            with pe.Fori(1, GROUPS // 2 - 1) as i:
                step(2 * i + 1, 1)
                step(2 * i + 2, 0)
            step(GROUPS - 1, 1, ahead=False)
            last = GROUPS - 1
            weighted_sum(last - 1, 0, 2)
            weighted_sum(last - 1, 0, 3)
            transpose_probs(last, 1, 0, ahead=False)
            transpose_probs(last, 1, 1, ahead=False)
            transpose_back(last - 1, 0, projected=False)
            transpose_back(last - 1, 1, projected=False)
            weighted_sum(last, 1, 0)
            weighted_sum(last, 1, 1)
            transpose_probs(last, 1, 2, ahead=False)
            transpose_probs(last, 1, 3, ahead=False)
            weighted_sum(last, 1, 2)
            weighted_sum(last, 1, 3)
            transpose_back(last, 0, projected=False)
            transpose_back(last, 1, projected=False)


_INS = ["x", "L0_conv_w_qkv", "L0_conv_b_qkv"]
_OUT = (B, C, H, W)


def kernel(**inputs):
    import numpy as _np
    import concourse.bacc as _bacc
    from concourse.bass_utils import run_bass_kernel_spmd as _run

    nc = _bacc.Bacc("TRN2", target_bir_lowering=False, num_devices=1)
    arrays, args = {}, []
    for name in _INS:
        a = _np.ascontiguousarray(inputs[name])
        arrays[f"in_{name}_dram"] = a
        args.append(nc.dram_tensor(f"in_{name}_dram", a.shape, mybir.dt.from_np(a.dtype), kind="ExternalInput").ap())
    args.append(nc.dram_tensor("out_dram", _OUT, mybir.dt.float32, kind="ExternalOutput").ap())
    window_attention(nc, *args)
    r = _run(nc, [arrays], core_ids=[0])
    return r.results[0]["out_dram"]
```

```python
import numpy as np

import concourse.bass as bass
from concourse import mybir
from contextlib import ExitStack

B, C, H, W = 4, 128, 112, 112
WS, SHIFT, HEADS, GN_GROUPS = 7, 3, 8, 32
HD = C // HEADS
PER = C // GN_GROUPS
EPS = 1e-5
TOK = WS * WS
BANDS = H // WS
NW = W // WS
GW = NW // 2
GT = GW * TOK
PAIRS = GW // 2
HP = HEADS // 2
PC = 2 * HD
ROWS2 = 2 * TOK
PITCH = 64
KROWS = PITCH + TOK
BAND = WS * W
SLOTS = 2 * BANDS
GROUPS = B * BANDS * 2
STAT = 448
CHUNKS = H * W // STAT
Q_LEN = GW * ROWS2
Q_PAD = 128 - ROWS2
PIECES = 7
NEWTON = 3
X_SCALE, W_SCALE = 8.0, 256.0
QK_SCALE = 1.0 / 16


def window_attention(nc, x, w_qkv, b_qkv, out):
    f32, f16, i32 = mybir.dt.float32, mybir.dt.float16, mybir.dt.int32
    ALU, ACT, AX = mybir.AluOpType, mybir.ActivationFunctionType, mybir.AxisListType

    x_v = x.rearrange("b c h w -> b c (h w)")
    out_v = out.rearrange("b c h w -> b c (h w)")

    ctx = ExitStack()
    with ctx:
        def sb(name, shape, dt=f32):
            return ctx.enter_context(nc.sbuf_tensor(name, shape, dt))

        def sem(name):
            return ctx.enter_context(nc.semaphore(name))

        image = sb("image", [C, SLOTS * BAND])
        xn = sb("xn", [C, GW, TOK])
        xn_hi, xn_lo = sb("xn_hi", [C, 2, GW, PITCH], f16), sb("xn_lo", [C, 2, GW, PITCH], f16)
        k32 = sb("k32", [C, GT])
        q32 = sb("q32", [C, GW, 2, TOK])
        k_hi, k_lo = sb("k_hi", [C, 2, GT], f16), sb("k_lo", [C, 2, GT], f16)
        q_hi, q_lo = sb("q_hi", [C, 2, Q_LEN + Q_PAD], f16), sb("q_lo", [C, 2, Q_LEN + Q_PAD], f16)
        row_max = sb("row_max", [ROWS2, 2, 2, GW])
        shifted = sb("shifted", [ROWS2, 2, 2, GW, TOK])
        probs = sb("probs", [ROWS2, 2, HP, GW, PITCH])
        probs_t = sb("probs_t", [KROWS, 2, HP, ROWS2])
        v_rows = sb("v_rows", [KROWS, 2, PAIRS, HP, 2, PC + 1])
        inv_sum = sb("inv_sum", [ROWS2, 2, 2, HP * 2])
        mixed = sb("mixed", [ROWS2, PAIRS, 2, HP, PC])
        even_out = sb("even_out", [C, 2, GW // 2, TOK])
        both_out = sb("both_out", [C, GW, TOK])
        stage = sb("stage", [C, 2 * BAND])
        w_nat = sb("w_nat", [C, 3, C])
        w_t = sb("w_t", [C, 3, C])
        w_hi, w_lo = sb("w_hi", [C, 3, C], f16), sb("w_lo", [C, 3, C], f16)
        bias = sb("bias", [C, 3])
        ident = sb("ident", [C, C])
        head_of = sb("head_of", [C, HEADS])
        even_odd = sb("even_odd", [C, 2])
        size = sb("size", [C, 3])
        size_b = sb("size_b", [C, 3])
        size_all = sb("size_all", [C, 3])
        fit = sb("fit", [C, 3])
        qk_fit = sb("qk_fit", [C, 2])
        q_scale, q_bias = sb("q_scale", [C, 2]), sb("q_bias", [C, 2])
        v_scale = sb("v_scale", [C, 2])
        k_bias = sb("k_bias", [C, 1])
        exp_scale = sb("exp_scale", [C, 1])
        stats = sb("stats", [C, CHUNKS, 6])
        mean_blk, var_blk = sb("mean_blk", [C, 32]), sb("var_blk", [C, 32])
        mean_row, var_row = sb("mean_row", [C, 32]), sb("var_row", [C, 32])
        work_a, work_b = sb("work_a", [C, 32]), sb("work_b", [C, 32])
        g_sum, g_var, rs, rs_t = (sb(n, [C, 8]) for n in ("g_sum", "g_var", "rs", "rs_t"))
        half_bits = sb("half_bits", [C, 8], i32)
        agg = sb("agg", [C, 2])
        mean_c, rstd_c = sb("mean_c", [C, 32]), sb("rstd_c", [C, 32])

        psum = ctx.enter_context(nc.psum_tensor("psum", [128, 8, 512], f32))
        S_BANKS, T_BANKS, PV_BANKS = slice(0, 2), (3, 2), slice(4, 6)
        K_BANK, Q_BANK, V_BANK, BACK_BANKS = 2, 6, 7, (6, 7)

        loaded0 = [sem(f"loaded_first_{n}") for n in range(PIECES)]
        loaded = [None] + [sem(f"loaded_image_{b}") for b in range(1, B)]
        w_loaded, stored = sem("w_loaded"), sem("stored")
        consts, sized, fitted, w_transposed = (sem(n) for n in ("consts", "sized", "fitted", "w_transposed"))
        w_scaled, w_split, scales_ready = (sem(n) for n in ("w_scaled", "w_split", "scales_ready"))
        pool_chain, dve_chain, agg_chain = sem("pool_chain"), sem("dve_chain"), sem("agg_chain")
        stats_done, waited, waited_sp = sem("stats_done"), sem("waited"), sem("waited_sp")
        x_high, x_split = sem("x_high"), sem("x_split")
        xn_ready, q_mm, k_mm, v_mm = sem("xn_ready"), sem("q_mm"), sem("k_mm"), sem("v_mm")
        q_evac, k_evac, v_evac = sem("q_evac"), sem("k_evac"), sem("v_evac")
        k_high, q_high, k_split, q_split = sem("k_high"), sem("q_high"), sem("k_split"), sem("q_split")
        s_mm = [sem("s_mm_0"), sem("s_mm_1")]
        max_done = [sem("max_done_0"), sem("max_done_1")]
        sub_done = [sem("sub_done_0"), sem("sub_done_1")]
        exp_done = [sem("exp_done_0"), sem("exp_done_1")]
        pt_mm, pt_evac, pv_mm = sem("pt_mm"), sem("pt_evac"), sem("pv_mm")
        inv_done, norm_done = sem("inv_done"), sem("norm_done")
        back_mm, even_done, both_done, add_done = sem("back_mm"), sem("even_done"), sem("both_done"), sem("add_done")

        def wait(engine, semaphore, count):
            if not isinstance(count, int) or count > 0:
                engine.wait_ge(semaphore, count)

        def in_windows(flat, first, n):
            rows = flat.rearrange("p (r c) -> p r c", c=W)[:, :, first:first + n * WS]
            return rows.rearrange("p r (w c) -> p w r c", c=WS)

        def pieces(half):
            if half == 0:
                return [(0, GW, 0, WS, SHIFT)]
            first = SHIFT + GW * WS
            return [(0, GW - 1, 0, WS, first), (GW - 1, 1, 0, WS - SHIFT, W - (WS - SHIFT)), (GW - 1, 1, WS - SHIFT, SHIFT, 0)]

        def token_view(tokens, piece):
            w0, n, c0, nc_, _ = piece
            return tokens[:, w0:w0 + n, :].rearrange("p w (r c) -> p w r c", c=WS)[:, :, :, c0:c0 + nc_]

        def pixel_view(flat, piece):
            w0, n, c0, nc_, first = piece
            if n > 1:
                return in_windows(flat, first, n)
            rows = flat.rearrange("p (r c) -> p r c", c=W)[:, :, first:first + nc_]
            return rows.rearrange("p r (w c) -> p w r c", c=nc_)

        block = ctx.enter_context(nc.Block())

        @block.sync
        def _(sp):
            sp.dma_start(w_nat[:, :, :], w_qkv.rearrange("(j o) c -> o j c", j=3)).then_inc(w_loaded, 16)
            sp.dma_start(bias[:, :], b_qkv.rearrange("(j o) -> o j", j=3), allow_slow_non_contiguous=True).then_inc(w_loaded, 16)

            def load_rows(b, row, n, semaphore, slot_row):
                sp.dma_start(image[:, slot_row * W:(slot_row + n) * W],
                             x_v[b, :, row * W:(row + n) * W]).then_inc(semaphore, 16)

            rows = H // PIECES
            for n in range(PIECES - 1):
                load_rows(0, n * rows + SHIFT, rows, loaded0[n], n * rows)
            load_rows(0, H - rows + SHIFT, rows - SHIFT, loaded0[PIECES - 1], H - rows)
            load_rows(0, 0, SHIFT, loaded0[PIECES - 1], H - SHIFT)
            load_rows(1, SHIFT, H - SHIFT, loaded[1], H)
            load_rows(1, 0, SHIFT, loaded[1], 2 * H - SHIFT)

            def store_band(b, y):
                t = b * BANDS + y
                sp.wait_ge(add_done, 2 * t + 2)
                sp.sem_inc(waited_sp, 1)
                at = (y & 1) * BAND
                top = (WS - SHIFT) * W
                src = stage[:, bass.ds(at, BAND)]
                sp.dma_start(out_v[bass.ds(b, 1), :, bass.ds((y * WS + SHIFT) * W, top)].rearrange("b c n -> c (b n)"),
                             src[:, 0:top]).then_inc(stored, 16)
                sp.dma_start(out_v[bass.ds(b, 1), :, bass.ds(((y + 1) & (BANDS - 1)) * BAND, BAND - top)]
                             .rearrange("b c n -> c (b n)"), src[:, top:BAND]).then_inc(stored, 16)

            def load_band(b_static, y):
                at = (b_static % 2) * BANDS * BAND + y * BAND
                top = (WS - SHIFT) * W
                slot = image[:, bass.ds(at, BAND)]
                sp.dma_start(slot[:, 0:top], x_v[b_static, :, bass.ds((y * WS + SHIFT) * W, top)]).then_inc(loaded[b_static], 16)
                sp.dma_start(slot[:, top:BAND], x_v[b_static, :, bass.ds(((y + 1) & (BANDS - 1)) * BAND, BAND - top)]
                             ).then_inc(loaded[b_static], 16)

            def wait_stored(b, y):
                sp.wait_ge(stored, 32 * (b * BANDS + y) + 32)
                sp.sem_inc(waited_sp, 1)

            for b in range(2):
                with sp.Fori(0, BANDS) as y:
                    store_band(b, y)
                    load_band(b + 2, y)
                    sp.wait_ge(loaded[b + 2], 32 * y + 32)
                    wait_stored(b, y)
            with sp.Fori(2, B) as b:
                with sp.Fori(0, BANDS) as y:
                    store_band(b, y)
                    wait_stored(b, y)

        @block.gpsimd
        def _(pool):
            nc.gpsimd.memset(ident[:, :], 0.0).then_inc(pool_chain, 1)
            nc.gpsimd.memset(head_of[:, :], 1.0).then_inc(pool_chain, 1)
            pool.wait_ge(pool_chain, 2)
            nc.gpsimd.affine_select(out=ident[:, :], in_=ident[:, :], compare_op=ALU.not_equal, fill=1.0, base=0,
                                    pattern=[[-1, C]], channel_multiplier=1).then_inc(consts, 1)
            nc.gpsimd.affine_select(out=head_of[:, :], in_=head_of[:, :], compare_op=ALU.is_ge, fill=0.0, base=0,
                                    pattern=[[-HD, HEADS]], channel_multiplier=1).then_inc(pool_chain, 1)
            pool.wait_ge(pool_chain, 3)
            nc.gpsimd.affine_select(out=head_of[:, :], in_=head_of[:, :], compare_op=ALU.is_ge, fill=0.0, base=HD - 1,
                                    pattern=[[HD, HEADS]], channel_multiplier=-1).then_inc(consts, 1)
            nc.gpsimd.memset(probs[:, :, :, :, TOK:PITCH], 0.0).then_inc(consts, 1)
            nc.gpsimd.memset(q_hi[:, :, Q_LEN:], 0.0).then_inc(consts, 1)
            nc.gpsimd.memset(q_lo[:, :, Q_LEN:], 0.0).then_inc(consts, 1)
            nc.gpsimd.memset(v_rows[:, :, :, :, :, :], 0.0).then_inc(pool_chain, 1)
            pool.wait_ge(pool_chain, 4)
            nc.gpsimd.memset(v_rows[0:TOK, :, :, :, 0, PC:PC + 1], 1.0).then_inc(consts, 1)
            nc.gpsimd.memset(v_rows[PITCH:KROWS, :, :, :, 1, PC:PC + 1], 1.0).then_inc(consts, 1)
            pool.wait_ge(sized, 1)
            pool.wait_ge(consts, 7)
            nc.gpsimd.partition_all_reduce(size_all[:, :], size[:, :], C, bass.bass_isa.ReduceOp.max).then_inc(consts, 1)
            pool.wait_ge(w_scaled, 6)
            nc.gpsimd.tensor_tensor(w_lo[:, :, :], w_t[:, :, :], w_hi[:, :, :], ALU.subtract).then_inc(w_split, 1)

            def split_x(g, par):
                wait(pool, v_mm, g - 1)
                pool.wait_ge(xn_ready, g + 1)
                pool.sem_inc(waited, 1)
                nc.gpsimd.tensor_scalar(xn_hi[:, par, :, 0:TOK], xn[:, :, :], 1.0, 0.0, ALU.mult, ALU.add).then_inc(x_high, 1)
                pool.wait_ge(x_high, g + 1)
                nc.gpsimd.tensor_tensor(xn_lo[:, par, :, 0:TOK], xn[:, :, :], xn_hi[:, par, :, 0:TOK],
                                        ALU.subtract).then_inc(x_split, 1)

            def split(g, par):
                pool.wait_ge(k_evac, g + 1)
                wait(pool, s_mm[1], g - 1)
                pool.sem_inc(waited, 1)
                nc.gpsimd.tensor_scalar(k_hi[:, par, :], k32[:, :], 1.0, 0.0, ALU.mult, ALU.add).then_inc(k_high, 1)
                pool.wait_ge(k_high, g + 1)
                nc.gpsimd.tensor_tensor(k_lo[:, par, :], k32[:, :], k_hi[:, par, :], ALU.subtract).then_inc(k_split, 1)
                pool.wait_ge(q_evac, g + 1)
                q_flat = q32[:, :, :, :].rearrange("p w e q -> p (w e q)")
                pool.sem_inc(waited, 1)
                nc.gpsimd.tensor_scalar(q_hi[:, par, 0:Q_LEN], q_flat, 1.0, 0.0, ALU.mult, ALU.add).then_inc(q_high, 1)
                pool.wait_ge(q_high, g + 1)
                nc.gpsimd.tensor_tensor(q_lo[:, par, 0:Q_LEN], q_flat, q_hi[:, par, 0:Q_LEN], ALU.subtract).then_inc(q_split, 1)

            def add_image(g, t, half):
                pool.wait_ge(both_done, 2 * g + 2)
                if half == 0:
                    wait(pool, stored, 32 * (t - 1))
                at, st = (t & (SLOTS - 1)) * BAND, (t & 1) * BAND
                for piece in pieces(half):
                    last = nc.gpsimd.tensor_tensor(pixel_view(stage[:, bass.ds(st, BAND)], piece), token_view(both_out, piece),
                                                   pixel_view(image[:, bass.ds(at, BAND)], piece), ALU.add)
                last.then_inc(add_done, 1)

            split_x(0, 0)
            split_x(1, 1)
            split(0, 0)
            split(1, 1)
            split_x(2, 0)
            split(2, 0)
            split_x(3, 1)

            def two_steps(i):
                split(2 * i + 3, 1)
                split_x(2 * i + 4, 0)
                add_image(2 * i, i, 0)
                split(2 * i + 4, 0)
                split_x(2 * i + 5, 1)
                add_image(2 * i + 1, i, 1)

            two_steps(0)
            two_steps(1)
            with pool.Fori(2, GROUPS // 2 - 2) as i:
                two_steps(i)
            split(GROUPS - 1, 1)
            for g in range(GROUPS - 4, GROUPS):
                add_image(g, g // 2, g % 2)

        @block.scalar
        def _(act):
            act.wait_ge(fitted, 1)
            act.wait_ge(w_transposed, 1)
            for w in (w_hi, w_t):
                for n in range(3):
                    nc.scalar.activation(w[:, n, :], psum[:, Q_BANK, n * C:(n + 1) * C], ACT.Identity,
                                         scale=fit[:, n:n + 1]).then_inc(w_scaled, 1)
            act.wait_ge(scales_ready, 1)

            def evac_qk(g):
                act.wait_ge(k_mm, g + 1)
                wait(act, k_split, g)
                nc.scalar.activation(k32[:, :], psum[:, K_BANK, 0:GT], ACT.Identity, bias=k_bias[:, 0:1],
                                     scale=QK_SCALE).then_inc(k_evac, 1)
                act.wait_ge(q_mm, g + 1)
                wait(act, q_split, g)
                q = psum[:, Q_BANK, 0:GT].rearrange("p (w q) -> p w q", q=TOK)
                for e in range(2):
                    last = nc.scalar.activation(q32[:, :, e, :], q, ACT.Identity, bias=q_bias[:, e:e + 1],
                                                scale=q_scale[:, e:e + 1])
                last.then_inc(q_evac, 1)

            def evac_probs_t(c, p):
                act.wait_ge(pt_mm, 4 * c + p + 1)
                wait(act, pv_mm, 4 * c + p - 1)
                nc.scalar.copy(probs_t[:, p % 2, :, :], psum[0:KROWS, T_BANKS[p % 2], 0:HP * ROWS2]
                               .rearrange("p (h q) -> p h q", h=HP)).then_inc(pt_evac, 1)

            def evac_v(g, par):
                act.wait_ge(v_mm, g + 1)
                wait(act, pv_mm, 4 * (g - 1))
                v = psum[:, V_BANK, :].rearrange("p (a h d) -> p a h d", a=PAIRS, h=HP)
                nc.scalar.copy(v_rows[0:TOK, par, :, :, 0, 0:PC], v[0:TOK])
                nc.scalar.copy(v_rows[PITCH:KROWS, par, :, :, 1, 0:PC], v[PITCH:KROWS]).then_inc(v_evac, 1)

            def exp(g, par, j):
                act.wait_ge(sub_done[j], g + 1)
                wait(act, pt_mm, 4 * (g - 1))
                nc.scalar.activation(probs[:, par, 2 * j:2 * j + 2, :, 0:TOK], shifted[:, j, :, :, :], ACT.Exp,
                                     scale=exp_scale[0:ROWS2, 0:1]).then_inc(exp_done[j], 1)

            def evac_back(c, n):
                act.wait_ge(back_mm, 2 * c + n + 1)
                wait(act, both_done, 2 * c + n - 1)
                back = psum[:, BACK_BANKS[n], 0:GW // 2 * ROWS2].rearrange("p (w e q) -> p w e q", e=2, q=TOK)
                nc.scalar.activation(even_out[:, n, :, :], back[:, :, 0, :], ACT.Identity, bias=bias[:, 2:3],
                                     scale=v_scale[:, 0:1]).then_inc(even_done, 1)

            def step(g, par, ahead=True, behind=2):
                if ahead:
                    evac_qk(g + 1)
                exp(g, par, 0)
                evac_v(g, par)
                if behind:
                    evac_probs_t(g - 1, 0)
                    evac_probs_t(g - 1, 1)
                if behind >= 2:
                    evac_back(g - 2, 0)
                    evac_back(g - 2, 1)
                if behind:
                    evac_probs_t(g - 1, 2)
                    evac_probs_t(g - 1, 3)
                exp(g, par, 1)

            evac_qk(0)
            step(0, 0, behind=0)
            step(1, 1, behind=1)
            step(2, 0)
            with act.Fori(1, GROUPS // 2 - 1) as i:
                step(2 * i + 1, 1)
                step(2 * i + 2, 0)
            step(GROUPS - 1, 1, ahead=False)
            evac_probs_t(GROUPS - 1, 0)
            evac_probs_t(GROUPS - 1, 1)
            evac_back(GROUPS - 2, 0)
            evac_back(GROUPS - 2, 1)
            evac_probs_t(GROUPS - 1, 2)
            evac_probs_t(GROUPS - 1, 3)
            evac_back(GROUPS - 1, 0)
            evac_back(GROUPS - 1, 1)

        @block.vector
        def _(dve):
            chained = [0]

            def chain(instruction):
                chained[0] += 1
                instruction.then_inc(dve_chain, 1)
                dve.wait_ge(dve_chain, chained[0])

            chain(nc.vector.memset(mean_blk[:, :], 0.0))
            chain(nc.vector.memset(var_blk[:, :], 0.0))
            chain(nc.vector.memset(xn_hi[:, :, :, TOK:PITCH], 0.0))
            chain(nc.vector.memset(xn_lo[:, :, :, TOK:PITCH], 0.0))
            dve.wait_ge(w_loaded, 32)
            chain(nc.vector.tensor_reduce(size[:, :], w_nat[:, :, :], AX.X, ALU.add, apply_absolute_value=True))
            chain(nc.vector.tensor_reduce(size_b[:, :], bias[:, :].rearrange("p (j o) -> p j o", o=1), AX.X, ALU.add,
                                          apply_absolute_value=True))
            nc.vector.tensor_tensor(size[:, :], size[:, :], size_b[:, :], ALU.add).then_inc(sized, 1)
            dve.wait_ge(consts, 8)
            chain(nc.vector.tensor_scalar(size_all[:, :], size_all[:, :], 1e-12, 1.0 / W_SCALE, ALU.max, ALU.mult))
            nc.vector.reciprocal(fit[:, :], size_all[:, :]).then_inc(fitted, 1)

            def work_out_scales():
                dve.wait_ge(fitted, 1)
                chain(nc.vector.tensor_reduce(even_odd[:, :], head_of[:, :].rearrange("p (h e) -> p e h", e=2), AX.X, ALU.add))
                nc.vector.tensor_scalar(q_scale[:, :], even_odd[:, :], QK_SCALE, None, ALU.mult)
                chain(nc.vector.tensor_scalar(qk_fit[:, :], fit[:, 0:2], X_SCALE * QK_SCALE, None, ALU.mult))
                nc.vector.tensor_scalar(q_bias[:, :], even_odd[:, :], bias[:, 0:1], qk_fit[:, 0:1], ALU.mult, ALU.mult)
                nc.vector.tensor_scalar(k_bias[:, :], qk_fit[:, 1:2], bias[:, 1:2], None, ALU.mult)
                nc.vector.tensor_scalar(v_scale[:, :], even_odd[:, :], size_all[:, 2:3], 1.0 / X_SCALE, ALU.mult, ALU.mult)
                chain(nc.vector.tensor_scalar(exp_scale[:, :], size_all[:, 0:1], size_all[:, 1:2], None, ALU.mult))
                nc.vector.tensor_scalar(exp_scale[:, :], exp_scale[:, :], float(HD) ** -0.5 / (X_SCALE * QK_SCALE) ** 2, None,
                                        ALU.mult).then_inc(scales_ready, 1)

            def take_stats(at, chunk):
                nc.vector.bn_stats(stats[:, bass.ds(chunk, 1), :].rearrange("p o s -> p (o s)"),
                                   image[:, bass.ds(at, STAT)]).then_inc(stats_done, 1)

            linked = [0]

            def link(instruction):
                linked[0] += 1
                instruction.then_inc(agg_chain, 1)
                dve.wait_ge(agg_chain, linked[0])

            def grouped(rows):
                return rows[:, :].rearrange("p (g c) -> p g c", c=PER)

            def gather_channels(b):
                dve.wait_ge(stats_done, CHUNKS * (b + 1))
                link(nc.vector.bn_aggr(agg[:, :], stats[:, :, :].rearrange("p n s -> p (n s)")))
                nc.vector.tensor_copy(mean_blk[:, 0:1], agg[:, 0:1])
                link(nc.vector.tensor_copy(var_blk[:, 0:1], agg[:, 1:2]))
                nc.vector.transpose(mean_row[:, :], mean_blk[:, :])
                link(nc.vector.transpose(var_row[:, :], var_blk[:, :]))
                link(nc.vector.tensor_reduce(g_sum[:, :], grouped(mean_row), AX.X, ALU.add))

            def group_variance():
                link(nc.vector.scalar_tensor_tensor(grouped(work_a), g_sum[:, :, None].broadcast_to([C, 8, PER]), -1.0 / PER,
                                                    grouped(mean_row), ALU.mult, ALU.add))
                link(nc.vector.tensor_tensor(work_b[:, :], work_a[:, :], work_a[:, :], ALU.mult))
                link(nc.vector.tensor_tensor(work_a[:, :], work_b[:, :], var_row[:, :], ALU.add))
                link(nc.vector.tensor_reduce(g_var[:, :], grouped(work_a), AX.X, ALU.add))
                link(nc.vector.tensor_scalar(g_var[:, :], g_var[:, :], 1.0 / PER, EPS, ALU.mult, ALU.add))

            def guess_root():
                link(nc.vector.tensor_scalar(half_bits[:, :], g_var[:, :].bitcast(i32), 1, None, ALU.logical_shift_right))
                link(nc.vector.tensor_scalar(rs[:, :].bitcast(i32), half_bits[:, :], -1.0, float(0x5F3759DF), ALU.mult, ALU.add))

            def refine_root(steps):
                for _ in range(steps):
                    link(nc.vector.tensor_tensor(rs_t[:, :], rs[:, :], rs[:, :], ALU.mult))
                    link(nc.vector.scalar_tensor_tensor(rs_t[:, :], rs_t[:, :], -0.5, g_var[:, :], ALU.mult, ALU.mult))
                    link(nc.vector.scalar_tensor_tensor(rs[:, :], rs_t[:, :], 1.5, rs[:, :], ALU.add, ALU.mult))

            def scatter_groups():
                refine_root(1)
                nc.vector.tensor_scalar(grouped(mean_row), g_sum[:, :, None].broadcast_to([C, 8, PER]), 1.0 / PER, None, ALU.mult)
                link(nc.vector.tensor_scalar(grouped(var_row), rs[:, :, None].broadcast_to([C, 8, PER]), X_SCALE, None, ALU.mult))
                nc.vector.transpose(mean_c[:, :], mean_row[:, :])
                link(nc.vector.transpose(rstd_c[:, :], var_row[:, :]))

            def normalise(g, t, half):
                wait(dve, x_split, g)
                at = (t & (SLOTS - 1)) * BAND
                for piece in pieces(half):
                    last = nc.vector.tensor_scalar(token_view(xn, piece),
                                                   pixel_view(image[:, bass.ds(at, BAND)], piece),
                                                   mean_c[:, 0:1], rstd_c[:, 0:1], ALU.subtract, ALU.mult)
                last.then_inc(xn_ready, 1)

            def maximum(g, j):
                dve.wait_ge(s_mm[j], g + 1)
                nc.vector.tensor_reduce(row_max[:, j, :, :], psum[0:ROWS2, S_BANKS, 0:GT]
                                        .rearrange("p h (w k) -> p h w k", k=TOK), AX.X, ALU.max).then_inc(max_done[j], 1)

            def subtract(g, j):
                dve.wait_ge(max_done[j], g + 1)
                wait(dve, exp_done[j], g)
                nc.vector.tensor_tensor(shifted[:, j, :, :, :], psum[0:ROWS2, S_BANKS, 0:GT]
                                        .rearrange("p h (w k) -> p h w k", k=TOK),
                                        row_max[:, j, :, :, None].broadcast_to([ROWS2, 2, GW, TOK]),
                                        ALU.subtract).then_inc(sub_done[j], 1)

            def divide(c, n):
                rows = psum[0:ROWS2, PV_BANKS, 0:HP * 2 * (PC + 1)].rearrange("p a (n d) -> p a n d", d=PC + 1)
                dve.wait_ge(pv_mm, 4 * c + 2 * n + 2)
                nc.vector.reciprocal(inv_sum[:, n, :, :], rows[:, :, :, PC]).then_inc(inv_done, 1)
                dve.wait_ge(inv_done, 2 * c + n + 1)
                wait(dve, back_mm, 2 * (c - 1) + n + 1)
                nc.vector.tensor_tensor(mixed[:, 2 * n:2 * n + 2, :, :, :].rearrange("p a w h d -> p a (w h) d"), rows[:, :, :, 0:PC],
                                        inv_sum[:, n, :, :, None].broadcast_to([ROWS2, 2, HP * 2, PC]), ALU.mult).then_inc(norm_done, 1)

            def join(c, n):
                dve.wait_ge(even_done, 2 * c + n + 1)
                wait(dve, add_done, c)
                back = psum[:, BACK_BANKS[n], 0:GW // 2 * ROWS2].rearrange("p (w e q) -> p w e q", e=2, q=TOK)
                nc.vector.scalar_tensor_tensor(both_out[:, GW // 2 * n:GW // 2 * (n + 1), :], back[:, :, 1, :],
                                               v_scale[:, 1:2], even_out[:, n, :, :], ALU.mult, ALU.add).then_inc(both_done, 1)

            def step(g, t2, par, chunks=(), image_at=None, ahead=True, behind=2, first=None, before=None, after=None):
                if first:
                    first()
                maximum(g, 0)
                subtract(g, 0)
                for chunk in chunks:
                    take_stats(image_at + chunk * STAT, chunk)
                if before:
                    before()
                if ahead:
                    normalise(g + 2, t2, par)
                if after:
                    after()
                if behind >= 2:
                    divide(g - 2, 1)
                maximum(g, 1)
                subtract(g, 1)
                if behind >= 2:
                    join(g - 2, 0)
                    join(g - 2, 1)
                if behind:
                    divide(g - 1, 0)

            def two_steps(i, chunk=None, image_at=None):
                step(2 * i + 1, i + 1, 1, () if chunk is None else (chunk,), image_at)
                step(2 * i + 2, i + 2, 0, () if chunk is None else (chunk + 1,), image_at)

            def change_image(b):
                i = b * BANDS - 3
                step(2 * i + 1, i + 1, 1, after=lambda: gather_channels(b))
                step(2 * i + 2, i + 2, 0, after=group_variance)
                step(2 * i + 3, i + 2, 1, first=guess_root, after=lambda: refine_root(1))
                step(2 * i + 4, i + 3, 0, first=lambda: refine_root(NEWTON - 2), before=scatter_groups)

            for n in range(PIECES):
                dve.wait_ge(loaded0[n], 16 if n < PIECES - 1 else 32)
                for chunk in range(n * CHUNKS // PIECES, (n + 1) * CHUNKS // PIECES):
                    take_stats(chunk * STAT, chunk)
            gather_channels(0)
            group_variance()
            guess_root()
            refine_root(NEWTON - 1)
            scatter_groups()
            normalise(0, 0, 0)
            work_out_scales()
            normalise(1, 0, 1)
            step(0, 1, 0, behind=0)
            dve.wait_ge(loaded[1], 32)
            step(1, 1, 1, (0, 1), BANDS * BAND, behind=1)
            step(2, 2, 0, (2, 3), BANDS * BAND)
            with dve.Fori(1, CHUNKS // 2 - 1) as i:
                two_steps(i, 2 * i + 2, BANDS * BAND)
            for b in (1, 2):
                change_image(b)
                at = ((b + 1) % 2) * BANDS * BAND
                first = b * BANDS - 1
                dve.wait_ge(loaded[b + 1], 32 * -(-2 * STAT // BAND))
                two_steps(first, 0, at)
                dve.wait_ge(loaded[b + 1], 32 * -(-4 * STAT // BAND))
                two_steps(first + 1, 2, at)
                dve.wait_ge(loaded[b + 1], 32 * BANDS)
                with dve.Fori(2, CHUNKS // 2) as n:
                    two_steps(n + first, 2 * n, at)
            change_image(B - 1)
            with dve.Fori((B - 1) * BANDS - 1, GROUPS // 2 - 2) as i:
                two_steps(i)
            step(GROUPS - 3, B * BANDS - 1, 1)
            step(GROUPS - 2, None, 0, ahead=False)
            step(GROUPS - 1, None, 1, ahead=False)
            divide(GROUPS - 2, 1)
            join(GROUPS - 2, 0)
            join(GROUPS - 2, 1)
            divide(GROUPS - 1, 0)
            divide(GROUPS - 1, 1)
            join(GROUPS - 1, 0)
            join(GROUPS - 1, 1)

        @block.tensor
        def _(pe):
            pe.wait_ge(w_loaded, 32)
            pe.wait_ge(consts, 8)
            for j in range(3):
                last = nc.tensor.transpose(psum[:, Q_BANK, j * C:(j + 1) * C], w_nat[:, j, :], ident[:, :])
            last.then_inc(w_transposed, 1)
            pe.wait_ge(w_scaled, 6)
            pe.wait_ge(w_split, 1)

            products = ((w_hi, xn_hi), (w_hi, xn_lo), (w_lo, xn_hi))

            def project_qk(g, par):
                pe.wait_ge(x_split, g + 1)
                if isinstance(g, int):
                    wait(pe, k_evac, g)
                wait(pe, pt_evac, 4 * (g - 2))
                for n, (w, xs) in enumerate(products):
                    last = nc.tensor.matmul(psum[:, K_BANK, 0:GT], w[:, 1, :], xs[:, par, :, 0:TOK], start=n == 0, stop=n == 2)
                last.then_inc(k_mm, 1)
                if isinstance(g, int):
                    wait(pe, q_evac, g)
                wait(pe, both_done, 2 * (g - 4) + 1)
                for n, (w, xs) in enumerate(products):
                    last = nc.tensor.matmul(psum[:, Q_BANK, 0:GT], w[:, 0, :], xs[:, par, :, 0:TOK], start=n == 0, stop=n == 2)
                last.then_inc(q_mm, 1)

            def project_v(g, par):
                if isinstance(g, int):
                    wait(pe, v_evac, g)
                wait(pe, both_done, 2 * (g - 3) + 2)
                for p in range(PAIRS):
                    for n, (w, xs) in enumerate(products):
                        last = nc.tensor.matmul(psum[:, V_BANK, p * C:(p + 1) * C],
                                                xs[:, par, 2 * p:2 * p + 2, :].rearrange("p w k -> p (w k)"),
                                                w[:, 2, :], start=n == 0, stop=n == 2, skip_group_check=True)
                last.then_inc(v_mm, 1)

            def scores(g, par, j):
                if j == 0:
                    pe.wait_ge(k_split, g + 1)
                    pe.wait_ge(q_split, g + 1)
                wait(pe, sub_done[1 - j], g + j)
                for w in range(GW):
                    for n, (q, k) in enumerate(((q_hi, k_hi), (q_hi, k_lo), (q_lo, k_hi))):
                        for h in (2 * j, 2 * j + 1):
                            rows = slice(h * PC, (h + 1) * PC)
                            last = nc.tensor.matmul(psum[:, h - 2 * j, w * TOK:(w + 1) * TOK], q[rows, par, w * ROWS2:w * ROWS2 + 128],
                                                    k[rows, par, w * TOK:(w + 1) * TOK], start=n == 0,
                                                    stop=n == 2, skip_group_check=True)
                last.then_inc(s_mm[j], 1)

            def wait_to_transpose(c, p, ahead):
                if p == 0:
                    pe.wait_ge(exp_done[0], c + 1)
                    pe.wait_ge(exp_done[1], c + 1)
                    wait(pe, pt_evac, 4 * c - 1)
                elif p == 1:
                    if ahead:
                        pe.wait_ge(k_evac, c + 3)
                    else:
                        pe.wait_ge(pt_evac, 4 * c)
                else:
                    pe.wait_ge(pt_evac, 4 * c + p - 1)

            def wait_to_sum(c, p):
                pe.wait_ge(pt_evac, 4 * c + p + 1)
                pe.wait_ge(v_evac, c + 1)
                wait(pe, norm_done, 2 * c + p // 2)

            def sum_and_transpose(weighted=None, probs_of=None, ahead=True):
                if probs_of:
                    wait_to_transpose(probs_of[0], probs_of[2], ahead)
                if weighted:
                    wait_to_sum(weighted[0], weighted[2])
                for h in range(HP):
                    if probs_of:
                        _, par, p = probs_of
                        transposed = nc.tensor.transpose(psum[0:KROWS, T_BANKS[p % 2], h * ROWS2:(h + 1) * ROWS2],
                                                         probs[:, par, h, 2 * p:2 * p + 2, :]
                                                         .rearrange("p w k -> p (w k)")[:, 0:KROWS], ident[0:ROWS2, 0:ROWS2])
                    if weighted:
                        _, par, p = weighted
                        sums = psum[0:ROWS2, PV_BANKS.start + p % 2, 0:2 * HP * (PC + 1)].rearrange("p (w h d) -> p w h d", w=2, h=HP)
                        summed = nc.tensor.matmul(sums[:, :, h, :], probs_t[:, p % 2, h, :], v_rows[:, par, p, h, :, :],
                                                  start=True, stop=True, skip_group_check=True)
                if probs_of:
                    transposed.then_inc(pt_mm, 1)
                if weighted:
                    summed.then_inc(pv_mm, 1)

            def transpose_back(c, n, projected=True):
                if not projected:
                    pe.wait_ge(both_done, 2 * c + n - 1)
                elif n == 0:
                    pe.wait_ge(q_evac, c + 4)
                else:
                    pe.wait_ge(v_evac, c + 3)
                pe.wait_ge(norm_done, 2 * c + n + 1)
                for w in range(GW // 2):
                    last = nc.tensor.transpose(psum[:, BACK_BANKS[n], w * ROWS2:(w + 1) * ROWS2],
                                               mixed[:, 2 * n + w // 2, w % 2, :, :].rearrange("p h d -> p (h d)"),
                                               ident[0:ROWS2, 0:ROWS2])
                last.then_inc(back_mm, 1)

            def step(g, par, ahead=True, behind=2):
                if behind:
                    scores(g, par, 0)
                if ahead:
                    project_qk(g + 1, 1 - par)
                project_v(g, par)
                if behind >= 2:
                    sum_and_transpose((g - 2, par, 2), (g - 1, 1 - par, 0))
                    sum_and_transpose((g - 2, par, 3), (g - 1, 1 - par, 1), ahead)
                elif behind:
                    sum_and_transpose(None, (g - 1, 1 - par, 0))
                    sum_and_transpose(None, (g - 1, 1 - par, 1))
                else:
                    scores(g, par, 0)
                scores(g, par, 1)
                if behind >= 2:
                    transpose_back(g - 2, 0, ahead)
                    transpose_back(g - 2, 1)
                if behind:
                    sum_and_transpose((g - 1, 1 - par, 0), (g - 1, 1 - par, 2))
                    sum_and_transpose((g - 1, 1 - par, 1), (g - 1, 1 - par, 3))

            project_qk(0, 0)
            step(0, 0, behind=0)
            step(1, 1, behind=1)
            step(2, 0)
            with pe.Fori(1, GROUPS // 2 - 1) as i:
                step(2 * i + 1, 1)
                step(2 * i + 2, 0)
            step(GROUPS - 1, 1, ahead=False)
            last = GROUPS - 1
            sum_and_transpose((last - 1, 0, 2))
            sum_and_transpose((last - 1, 0, 3))
            sum_and_transpose(None, (last, 1, 0), ahead=False)
            sum_and_transpose(None, (last, 1, 1), ahead=False)
            transpose_back(last - 1, 0, projected=False)
            transpose_back(last - 1, 1, projected=False)
            sum_and_transpose((last, 1, 0), (last, 1, 2))
            sum_and_transpose((last, 1, 1), (last, 1, 3))
            sum_and_transpose((last, 1, 2))
            sum_and_transpose((last, 1, 3))
            transpose_back(last, 0, projected=False)
            transpose_back(last, 1, projected=False)


_INS = ["x", "L0_conv_w_qkv", "L0_conv_b_qkv"]
_OUT = (B, C, H, W)


def kernel(**inputs):
    import numpy as _np
    import concourse.bacc as _bacc
    from concourse.bass_utils import run_bass_kernel_spmd as _run

    nc = _bacc.Bacc("TRN2", target_bir_lowering=False, num_devices=1)
    arrays, args = {}, []
    for name in _INS:
        a = _np.ascontiguousarray(inputs[name])
        arrays[f"in_{name}_dram"] = a
        args.append(nc.dram_tensor(f"in_{name}_dram", a.shape, mybir.dt.from_np(a.dtype), kind="ExternalInput").ap())
    args.append(nc.dram_tensor("out_dram", _OUT, mybir.dt.float32, kind="ExternalOutput").ap())
    window_attention(nc, *args)
    r = _run(nc, [arrays], core_ids=[0])
    return r.results[0]["out_dram"]
```
